# Optimizing a Trainium2 kernel written in Bass

```python
import numpy as np
import jax
import jax.numpy as jnp

def _softmax(x, axis=-1):
    return jax.nn.softmax(x, axis=axis)

def _gelu(x):
    return jax.nn.gelu(x, approximate=True)

def _silu(x):
    return jax.nn.silu(x)

def _sigmoid(x):
    return jax.nn.sigmoid(x)

def _layernorm(x, axis=-1, eps=1e-05):
    m = jnp.mean(x, axis=axis, keepdims=True)
    v = jnp.var(x, axis=axis, keepdims=True)
    return (x - m) / jnp.sqrt(v + eps)

def _scatter_add(tgt, idx, src, axis=0):
    return tgt.at[idx].add(src)

def _segment_sum(src, seg, n):
    return jax.ops.segment_sum(src, seg, n)
kernel_name = 'mk_adaln_d1_jaxref_r8_531f03'

def setup_inputs(seed: int=0):
    np.random.seed(seed)
    _w = jnp.asarray

    def _L0_attn_setup():
        import jax, jax.numpy as jnp
        import numpy as np
        B, T, C = (8, 256, 128)
        H = 4 * C
        N_LAYER, LAYER_ID = (12, 2)
        K_CLAMP = 60.0
        LN_EPS = 1e-05

        def _ln(x, g, b):
            m = jnp.mean(x, axis=-1, keepdims=True)
            v = jnp.var(x, axis=-1, keepdims=True)
            return (x - m) * jax.lax.rsqrt(v + LN_EPS) * g + b

        def _mix(x, time_mix, combined_mix):
            c = x.shape[-1]
            xm1 = jnp.pad(x[:, :-1], ((0, 0), (1, 0), (0, 0)))
            xp1 = jnp.pad(x[:, 1:], ((0, 0), (0, 1), (0, 0)))
            xc = jnp.concatenate([xm1[..., :c // 2], xp1[..., c // 2:]], axis=-1)
            return x * time_mix + xm1 * (1.0 - time_mix) + xc * combined_mix

        def _wkv(time_decay, time_first, k, v):
            ed = jnp.exp(-jnp.exp(time_decay))
            eu = jnp.exp(time_first)

            def step(carry, kv_t):
                a, b = carry
                kt, vt = kv_t
                y = (a + eu * kt * vt) / (b + eu * kt)
                return ((ed * a + kt * vt, ed * b + kt), y)
            kT = jnp.swapaxes(k, 0, 1)
            vT = jnp.swapaxes(v, 0, 1)
            z = jnp.zeros_like(kT[0])
            _, y = jax.lax.scan(step, (z, z), (kT, vT))
            return jnp.swapaxes(y, 0, 1)

        def _time_mix_block(x, time_mix, combined_mix, time_decay, time_first, Wk, Wv, Wr, Wo):
            xm = _mix(x, time_mix, combined_mix)
            k = jnp.exp(jnp.minimum(xm @ Wk.T, K_CLAMP))
            v = xm @ Wv.T
            r = xm @ Wr.T
            wkv = _wkv(time_decay, time_first, k, v)
            return jax.nn.sigmoid(r) * wkv @ Wo.T

        def _channel_mix_block(x, time_mix, combined_mix, Fk, Fv, Fr):
            xm = _mix(x, time_mix, combined_mix)
            k = jnp.square(jax.nn.relu(xm @ Fk.T))
            kv = k @ Fv.T
            return jax.nn.sigmoid(xm @ Fr.T) * kv
        key = jax.random.key(seed)
        ks = jax.random.split(key, 9)
        s = 0.02
        x = jax.random.normal(ks[0], (B, T, C), jnp.float32)
        h = np.arange(C, dtype=np.float64)
        frac = (LAYER_ID - 1) / (N_LAYER - 2)
        f1 = 3.0 + frac * (1.2 - 3.0)
        f2 = 0.65 + frac * (0.4 - 0.65)
        decay_speed = np.power(f2, h / (C - 1) * 7.0) * f1
        tm = jnp.concatenate([jnp.zeros(C // 2), jnp.ones(C // 2)]).reshape(1, 1, C).astype(jnp.float32)
        return dict(x=x, ln1_g=jnp.ones((C,), jnp.float32), ln1_b=jnp.zeros((C,), jnp.float32), ln2_g=jnp.ones((C,), jnp.float32), ln2_b=jnp.zeros((C,), jnp.float32), att_time_mix=tm, att_combined_mix=jnp.full((1, 1, C), 0.01, jnp.float32), time_decay=jnp.asarray(np.log(decay_speed), jnp.float32), time_first=jnp.full((C,), float(np.log(0.3)), jnp.float32), Wk=jax.random.normal(ks[1], (C, C), jnp.float32) * s, Wv=jax.random.normal(ks[2], (C, C), jnp.float32) * s, Wr=jax.random.normal(ks[3], (C, C), jnp.float32) * s, Wo=jax.random.normal(ks[4], (C, C), jnp.float32) * s, ffn_time_mix=tm, ffn_combined_mix=jnp.full((1, 1, C), 0.01, jnp.float32), Fk=jax.random.normal(ks[5], (H, C), jnp.float32) * s, Fv=jax.random.normal(ks[6], (C, H), jnp.float32) * s, Fr=jax.random.normal(ks[7], (C, C), jnp.float32) * s)
    _L0_attn_in = _L0_attn_setup()

    def _L0_ffn_setup():
        import jax, jax.numpy as jnp
        import numpy as np
        E = 16
        H = 128
        F = 256
        TOP_K = 1
        B, S = (2, 128)
        key = jax.random.key(seed)
        ks = jax.random.split(key, 7)
        s = 0.02
        return {'hidden_states': jax.random.normal(ks[0], (B, S, H), jnp.float32), 'w_router': jax.random.normal(ks[1], (E, H), jnp.float32) * s, 'gate_up_proj': jax.random.normal(ks[2], (E, H, 2 * F), jnp.float32) * s, 'down_proj': jax.random.normal(ks[3], (E, F, H), jnp.float32) * s, 'w_gate': jax.random.normal(ks[4], (F, H), jnp.float32) * s, 'w_up': jax.random.normal(ks[5], (F, H), jnp.float32) * s, 'w_down': jax.random.normal(ks[6], (H, F), jnp.float32) * s}
    _L0_ffn_in = _L0_ffn_setup()
    _L0_c = _w((lambda *s: np.random.randn(*s).astype(np.float32) * 0.05)(8, 128))
    _L0_wmod = _w((lambda *s: np.random.randn(*s).astype(np.float32) * 0.05)(128, 6 * 128) * 128 ** (-0.5))
    _d = {'L0_attn_x': _L0_attn_in['x'], 'L0_attn_ln1_g': _L0_attn_in['ln1_g'], 'L0_attn_ln1_b': _L0_attn_in['ln1_b'], 'L0_attn_ln2_g': _L0_attn_in['ln2_g'], 'L0_attn_ln2_b': _L0_attn_in['ln2_b'], 'L0_attn_att_time_mix': _L0_attn_in['att_time_mix'], 'L0_attn_att_combined_mix': _L0_attn_in['att_combined_mix'], 'L0_attn_time_decay': _L0_attn_in['time_decay'], 'L0_attn_time_first': _L0_attn_in['time_first'], 'L0_attn_Wk': _L0_attn_in['Wk'], 'L0_attn_Wv': _L0_attn_in['Wv'], 'L0_attn_Wr': _L0_attn_in['Wr'], 'L0_attn_Wo': _L0_attn_in['Wo'], 'L0_attn_ffn_time_mix': _L0_attn_in['ffn_time_mix'], 'L0_attn_ffn_combined_mix': _L0_attn_in['ffn_combined_mix'], 'L0_attn_Fk': _L0_attn_in['Fk'], 'L0_attn_Fv': _L0_attn_in['Fv'], 'L0_attn_Fr': _L0_attn_in['Fr'], 'L0_ffn_w_router': _L0_ffn_in['w_router'], 'L0_ffn_gate_up_proj': _L0_ffn_in['gate_up_proj'], 'L0_ffn_down_proj': _L0_ffn_in['down_proj'], 'L0_ffn_w_gate': _L0_ffn_in['w_gate'], 'L0_ffn_w_up': _L0_ffn_in['w_up'], 'L0_ffn_w_down': _L0_ffn_in['w_down'], 'L0_c': _L0_c, 'L0_wmod': _L0_wmod}
    _x0 = _d['L0_attn_x']
    _d['L0_attn_x'] = jax.random.normal(jax.random.fold_in(jax.random.key(seed), 1), (8, 512, 128), dtype=_x0.dtype)
    del _x0
    return _d

def reference(L0_attn_x, L0_attn_ln1_g, L0_attn_ln1_b, L0_attn_ln2_g, L0_attn_ln2_b, L0_attn_att_time_mix, L0_attn_att_combined_mix, L0_attn_time_decay, L0_attn_time_first, L0_attn_Wk, L0_attn_Wv, L0_attn_Wr, L0_attn_Wo, L0_attn_ffn_time_mix, L0_attn_ffn_combined_mix, L0_attn_Fk, L0_attn_Fv, L0_attn_Fr, L0_ffn_w_router, L0_ffn_gate_up_proj, L0_ffn_down_proj, L0_ffn_w_gate, L0_ffn_w_up, L0_ffn_w_down, L0_c, L0_wmod):

    def _L0_attn_ref(x, ln1_g, ln1_b, ln2_g, ln2_b, att_time_mix, att_combined_mix, time_decay, time_first, Wk, Wv, Wr, Wo, ffn_time_mix, ffn_combined_mix, Fk, Fv, Fr):
        import jax, jax.numpy as jnp
        import numpy as np
        B, T, C = (8, 256, 128)
        H = 4 * C
        N_LAYER, LAYER_ID = (12, 2)
        K_CLAMP = 60.0
        LN_EPS = 1e-05

        def _ln(x, g, b):
            m = jnp.mean(x, axis=-1, keepdims=True)
            v = jnp.var(x, axis=-1, keepdims=True)
            return (x - m) * jax.lax.rsqrt(v + LN_EPS) * g + b

        def _mix(x, time_mix, combined_mix):
            c = x.shape[-1]
            xm1 = jnp.pad(x[:, :-1], ((0, 0), (1, 0), (0, 0)))
            xp1 = jnp.pad(x[:, 1:], ((0, 0), (0, 1), (0, 0)))
            xc = jnp.concatenate([xm1[..., :c // 2], xp1[..., c // 2:]], axis=-1)
            return x * time_mix + xm1 * (1.0 - time_mix) + xc * combined_mix

        def _wkv(time_decay, time_first, k, v):
            ed = jnp.exp(-jnp.exp(time_decay))
            eu = jnp.exp(time_first)

            def step(carry, kv_t):
                a, b = carry
                kt, vt = kv_t
                y = (a + eu * kt * vt) / (b + eu * kt)
                return ((ed * a + kt * vt, ed * b + kt), y)
            kT = jnp.swapaxes(k, 0, 1)
            vT = jnp.swapaxes(v, 0, 1)
            z = jnp.zeros_like(kT[0])
            _, y = jax.lax.scan(step, (z, z), (kT, vT))
            return jnp.swapaxes(y, 0, 1)

        def _time_mix_block(x, time_mix, combined_mix, time_decay, time_first, Wk, Wv, Wr, Wo):
            xm = _mix(x, time_mix, combined_mix)
            k = jnp.exp(jnp.minimum(xm @ Wk.T, K_CLAMP))
            v = xm @ Wv.T
            r = xm @ Wr.T
            wkv = _wkv(time_decay, time_first, k, v)
            return jax.nn.sigmoid(r) * wkv @ Wo.T

        def _channel_mix_block(x, time_mix, combined_mix, Fk, Fv, Fr):
            xm = _mix(x, time_mix, combined_mix)
            k = jnp.square(jax.nn.relu(xm @ Fk.T))
            kv = k @ Fv.T
            return jax.nn.sigmoid(xm @ Fr.T) * kv
        x = _ln(x, ln1_g, ln1_b)
        x = x + _time_mix_block(x, att_time_mix, att_combined_mix, time_decay, time_first, Wk, Wv, Wr, Wo)
        x = _ln(x, ln2_g, ln2_b)
        x = x + _channel_mix_block(x, ffn_time_mix, ffn_combined_mix, Fk, Fv, Fr)
        return x

    def _L0_ffn_ref(hidden_states, w_router, gate_up_proj, down_proj, w_gate, w_up, w_down):
        import jax, jax.numpy as jnp
        import numpy as np
        E = 16
        H = 128
        F = 256
        TOP_K = 1
        B, S = (2, 128)
        b, s, h = hidden_states.shape
        x = hidden_states.reshape(-1, h)
        logits = x @ w_router.T
        _, top_idx = jax.lax.top_k(logits, TOP_K)
        mask = jax.nn.one_hot(top_idx, E, dtype=logits.dtype).sum(axis=1)
        scores = jax.nn.sigmoid(logits) * mask
        masked_inputs = scores.T[:, :, None] * x[None, :, :]
        gate_up = jnp.einsum('eth,ehf->etf', masked_inputs, gate_up_proj)
        gate, up = jnp.split(gate_up, 2, axis=-1)
        expert_out = jnp.einsum('etf,efh->eth', up * jax.nn.silu(gate), down_proj)
        shared = jax.nn.silu(x @ w_gate.T) * (x @ w_up.T) @ w_down.T
        out = shared + expert_out.sum(axis=0)
        return out.reshape(b, s, h)
    x = L0_attn_x
    mod = (_silu(L0_c) @ L0_wmod).reshape(L0_c.shape[0], 6, 1, -1)
    sa, ca, ga, sb, cb, gb = (mod[:, 0], mod[:, 1], mod[:, 2], mod[:, 3], mod[:, 4], mod[:, 5])
    ga = (2 * (ga >= 0) - 1) * jnp.maximum(jnp.abs(ga), 0.25)
    gb = (2 * (gb >= 0) - 1) * jnp.maximum(jnp.abs(gb), 0.25)
    h = _layernorm(x, axis=-1) * (1 + ca) + sa
    x = x + ga * _L0_attn_ref(h, L0_attn_ln1_g, L0_attn_ln1_b, L0_attn_ln2_g, L0_attn_ln2_b, L0_attn_att_time_mix, L0_attn_att_combined_mix, L0_attn_time_decay, L0_attn_time_first, L0_attn_Wk, L0_attn_Wv, L0_attn_Wr, L0_attn_Wo, L0_attn_ffn_time_mix, L0_attn_ffn_combined_mix, L0_attn_Fk, L0_attn_Fv, L0_attn_Fr)
    h = _layernorm(x, axis=-1) * (1 + cb) + sb
    x = x + gb * _L0_ffn_ref(h, L0_ffn_w_router, L0_ffn_gate_up_proj, L0_ffn_down_proj, L0_ffn_w_gate, L0_ffn_w_up, L0_ffn_w_down)
    return x

_drawn_inputs = setup_inputs


def setup_inputs(seed=0):
    import zlib

    import numpy as np

    out = dict(_drawn_inputs(seed))
    spreads = {'L0_attn_ln1_g': (1.0, 0.2),
     'L0_attn_ln1_b': (0.0, 0.323),
     'L0_attn_ln2_g': (1.0, 0.2),
     'L0_attn_ln2_b': (0.0, 0.291),
     'L0_attn_att_combined_mix': (0.009999999776482582, 0.6),
     'L0_attn_time_first': (-1.2039728164672852, 0.6),
     'L0_attn_ffn_combined_mix': (0.009999999776482582, 0.6)}
    factors = {'L0_attn_att_time_mix': 8.0,
     'L0_attn_time_decay': 8.0,
     'L0_attn_Wk': 8.0,
     'L0_attn_Wv': 8.0,
     'L0_attn_Wr': 8.0,
     'L0_attn_Wo': 8.0,
     'L0_attn_ffn_time_mix': 8.0,
     'L0_attn_Fk': 8.0,
     'L0_attn_Fv': 8.0,
     'L0_attn_Fr': 8.0,
     'L0_ffn_w_router': 43.491,
     'L0_ffn_gate_up_proj': 42.292,
     'L0_ffn_down_proj': 42.191,
     'L0_ffn_w_gate': 42.604,
     'L0_ffn_w_up': 37.948,
     'L0_ffn_w_down': 37.884}
    for name, (base, spread) in spreads.items():
        noise = np.random.default_rng([zlib.crc32(name.encode()), seed]).standard_normal(out[name].shape)
        drawn = base * np.exp(spread * noise) if base else spread * noise
        out[name] = jnp.asarray(drawn.astype(out[name].dtype))
    for name, factor in factors.items():
        out[name] = (out[name] * factor).astype(out[name].dtype)
    return out
```

```python
import numpy as np


def program(nc, ins, out_t):
    import contextlib
    import concourse.bass as bass
    from concourse import mybir

    F32, I32, BF16 = mybir.dt.float32, mybir.dt.int32, mybir.dt.bfloat16
    ALU, ACT, AX = mybir.AluOpType, mybir.ActivationFunctionType, mybir.AxisListType

    NB, T, C = ins["x"].shape
    P = 128
    NT = T // P
    NTT = NB * NT
    PAIRS = NB // 2
    H = ins["FkT"].shape[1]
    HC = H // P
    E = ins["routerT"].shape[1]
    F = ins["gateT"].shape[1]
    FC = F // P
    NBLK = NTT + E - 1
    ROW = C + 4
    NOROW = NB * T
    LAG = 3
    DEPTH = 6
    DRAIN = 3
    EPS, KMAX = 1e-5, 60.0
    HALF = C // 2

    ctx = contextlib.ExitStack()
    with ctx:
        def sb(name, shape, dt=F32):
            return ctx.enter_context(nc.sbuf_tensor(name, shape, dt))

        ident = sb("ident", [P, P])
        identb = sb("ident_bf", [P, P], BF16)
        ones_bf = sb("ones_bf", [P, P], BF16)
        before_bf = sb("before_bf", [P, P], BF16)
        vecs = sb("vecs", [P, 10])
        derived = sb("derived", [P, 12])
        modc = sb("modc", [P, 6, NB])
        small = sb("small", [P, 48])
        cT = sb("cT", [P, NB])
        sc = sb("sc", [P, NB])
        ca_rows = sb("ca_rows", [P, NB, C])
        sa_rows = sb("sa_rows", [P, NB, C])
        decay = sb("decay", [P, T])
        Wk = sb("Wk", [P, C]); Wv = sb("Wv", [P, C]); Wr = sb("Wr", [P, C]); Wo = sb("Wo", [P, C])
        Fk = sb("Fk", [P, H]); Fv = sb("Fv", [P, HC, C]); Fr = sb("Fr", [P, C])
        Wg = sb("Wg", [P, F]); Wu = sb("Wu", [P, F]); Wd = sb("Wd", [P, FC, C])
        router = sb("router", [P, E])
        h2_all = sb("h2_all", [P, NB * T])
        x3_all = sb("x3_all", [P, NB * T])
        rows = sb("rows", [P, NTT, ROW])
        logits = sb("logits", [P, NTT, E])
        top = sb("top", [P, NTT])
        slot_i = sb("slot_i", [P, NTT], I32)
        block_expert = sb("block_expert", [1, NBLK + 1], I32)
        up_experts = sb("up_experts", [P, E, 2 * F])
        down_experts = sb("down_experts", [P, FC, E, C])

        WORK = 25 * (T + 8)
        work = sb("work", [P, WORK])
        at = [0]

        def carve(n):
            a = at[0]
            at[0] += n
            assert at[0] <= WORK, (at[0], WORK)
            return work[:, a:a + n]

        def two(n):
            return [carve(n), carve(n)]

        def tiles(ap):
            return ap.rearrange("p (j c) -> p j c", c=C)

        xtok, ht = tiles(carve(T)), tiles(carve(T))
        xT, xm, xm2 = carve(T), carve(T), carve(T)
        x1p, x2p = carve(T + 2), carve(T + 2)
        ek, er, kv, num, er2 = carve(T), carve(T), carve(T), carve(T), carve(T)
        apad, bpad = carve(T + 1), carve(T + 1)
        n3t, n4t = carve(T), carve(T)
        relus = [carve(T) for _ in range(2)]
        h2w, x3w = carve(T), carve(T)
        stat = [carve(6 * NT) for _ in range(4)]
        mv = [carve(2 * NT).rearrange("p (j s) -> p j s", s=2) for _ in range(4)]
        rstd = [carve(NT) for _ in range(4)]
        shift = [carve(NT) for _ in range(2)]
        eexp = carve(NT)
        neghalf = sb("neghalf", [P, NT])

        at[0] = 0
        G = NTT * E
        onehot = carve(G); rank = carve(G); total = carve(G); cum = carve(G); seg = carve(G); cand = carve(G)
        onehot_b = carve(G // 2).bitcast(BF16)
        blocks = carve(E * NTT); bend = carve(E); nblk = carve(E); bstart = carve(E); best = carve(NTT); slot_f = carve(NTT)
        iota_e = carve(G); iota_t = carve(NTT); ltmp = carve(NBLK * E); iota_blk = carve(NBLK * E); esum = carve(NBLK)
        ones_e = carve(E)
        sg = [[carve(T) for _ in range(FC)] for _ in range(2)]
        xb = [carve(ROW) for _ in range(DEPTH)]
        xbT = two(P)
        sge, acte, aT = two(F), two(F), two(F)
        yb = [carve(C) for _ in range(DEPTH)]
        number = [carve(1).bitcast(I32) for _ in range(DEPTH)]
        at[0] = 0
        yt = [tiles(t) for t in two(T)]; fin = two(T)
        pad_row = sb("pad_row", [P, ROW])

        bank = [ctx.enter_context(nc.psum_tensor(f"bank{n}", [P, 512], F32)) for n in range(8)]
        bT1, bK, bV, bR, bX2, bT2, bFR, bFK = range(8)
        bT3, bT4, bRT, bLG, bFV, bFK2 = bT1, bT1, bK, bR, bT2, bFR
        tok = lambda n: bank[n][:].rearrange("p (j c) -> p j c", c=C)
        sorted_rows = nc.dram_tensor("sorted_rows", [NBLK * P, ROW], F32, kind="Internal").ap()
        y_rows = nc.dram_tensor("y_rows", [NB * T, C], F32, kind="Internal").ap()

        lone_waits = [ctx.enter_context(nc.semaphore(f"lone_waits{n}")) for n in range(2)]
        gpsimd = [None]
        lifted = {"A_rs3": "pool", "A_t3": "pe", "A_rt": "pe", "A_rows": "dve", "E_f": "dve"}
        lifts = {e: [] for e in set(lifted.values())}

        def wait(eng, semaphore, value, alone=False):
            w = eng.wait_ge(semaphore, value)
            if not isinstance(value, int):
                if eng is gpsimd[0]:
                    w.then_inc(lone_waits[0], 1)
                elif alone:
                    w.then_inc(lone_waits[1], 1)

        class Steps:

            def __init__(self, name, n, slots=2, unit=1):
                self.n, self.unit, self.base = n * unit, unit, 0
                self.sem = [ctx.enter_context(nc.semaphore(f"{name}{q}")) for q in range(slots)]
                self.count = 0
                for key, e in lifted.items():
                    if name.startswith(key):
                        self.base = 1
                        lifts[e].append(self)

            def start(self, q, i):
                return i * self.n + self.base

            def lift(self, eng):
                assert self.base
                for s in self.sem:
                    eng.sem_inc(s, 1)

            def at(self, q):
                return self.sem[q]

            def begin(self, eng, q, i):
                self.eng, self.q, self.i, self.count = eng, q, i, 0
                return self

            def __call__(self, instruction, then_wait=False):
                self.count += self.unit
                assert self.count <= self.n
                instruction.then_inc(self.at(self.q), self.unit)
                if then_wait:
                    wait(self.eng, self.at(self.q), self.start(self.q, self.i) + self.count, then_wait == "alone")

            def done(self, eng, q, i, part=None):
                wait(eng, self.at(q), self.start(q, i) + (self.n if part is None else part * self.unit))

            def before(self, eng, q, i):
                if not (isinstance(i, int) and i == 0):
                    wait(eng, self.at(q), self.start(0, i))

        class Turns(Steps):

            def __init__(self, name, n, places=2):
                super().__init__(name, n, 1)
                self.places = places

            def start(self, q, i):
                return (self.places * i + q) * self.n + self.base

            def at(self, q):
                return self.sem[0]

        class Line(Steps):

            def __init__(self, name, n, unit=1):
                super().__init__(name, n, 1, unit)

            def begin(self, eng, b):
                return super().begin(eng, 0, b)

            def done(self, eng, b, part=None):
                super().done(eng, 0, b, part)

            def before(self, eng, b):
                super().before(eng, 0, b)

        def once(name, n, unit=1):
            return Steps(name, n, 1, unit)

        L_small = once("L_small", 3, 16)
        L_wmod = once("L_wmod", 1, 16)
        L_att = once("L_att", 4, 16)
        L_ffn = once("L_ffn", 3, 16)
        L_shared = once("L_shared", 4, 16)
        L_experts = once("L_experts", 3, 16)
        L_fill = once("L_fill", 1, 16)
        K_pool = once("K_pool", 15)
        K_dve = once("K_dve", 32)
        K_act = once("K_act", 5)
        K_pe = once("K_pe", 1 + NB // 2)
        K_rows = once("K_rows", NB // 2 * 2)
        A_x = Line("A_x", 1, unit=16)
        A_xT = Line("A_xT", 1, unit=16)
        A_st = [Line(f"A_st{n}_", 2 * NT) for n in range(4)]
        A_rs = [Line(f"A_rs{n}_", 2 if n < 2 else 4) for n in range(4)]
        A_n1 = Line("A_n1", NT)
        A_mod = Line("A_mod", 2)
        A_n2 = Line("A_n2", NT)
        A_t1 = Line("A_t1", 1)
        A_x1 = Line("A_x1", 2)
        A_mix = Line("A_mix", 2)
        A_kvr = Line("A_kvr", 3)
        A_exp = Line("A_exp", 2)
        A_wkv = Line("A_wkv", 8)
        A_cl = Line("A_cl", 1)
        A_wo = Line("A_wo", 1)
        A_n3 = Line("A_n3", NT)
        A_t2 = Line("A_t2", 1)
        A_x2 = Line("A_x2", 2)
        A_mix2 = Line("A_mix2", 2)
        A_fr = Line("A_fr", 1)
        A_fk = Line("A_fk", HC)
        A_relu = Line("A_relu", HC)
        A_sqa = Line("A_sqa", HC // 2)
        A_sqp = Line("A_sqp", HC // 2)
        A_fv = Line("A_fv", HC)
        A_th = Line("A_th", 1)
        A_x3 = Line("A_x3", 4)
        A_t3 = Line("A_t3", 1)
        A_n4 = Line("A_n4", NT)
        A_t4 = Line("A_t4", 1)
        A_h2 = Line("A_h2", 2)
        A_lg = Line("A_lg", 1)
        A_rt = Line("A_rt", 1)
        A_top = Line("A_top", 2)
        A_es = Line("A_es", 1)
        A_rows = Line("A_rows", 3)
        B_hot = once("B_hot", 5)
        B_cnt = once("B_cnt", 2)
        B_slot = once("B_slot", 21)
        B_pool = once("B_pool", 4)
        B_out = once("B_out", NTT, 16)
        C_gu = Turns("C_gu", 2 * FC)
        C_sg = Turns("C_sg", FC)
        C_act = Turns("C_act", FC)
        C_dn = Turns("C_dn", 1)
        C_base = Turns("C_base", 1)
        D_x = Steps("D_x", 1, DEPTH, 16)
        D_t = Turns("D_t", 1, DEPTH)
        D_xT = Turns("D_xT", 1, DEPTH)
        D_gu = Turns("D_gu", 1, DEPTH)
        D_sg = Turns("D_sg", 1, DEPTH)
        D_act = Turns("D_act", 2, DEPTH)
        D_at = Turns("D_at", 1, DEPTH)
        D_aT = Turns("D_aT", 1, DEPTH)
        D_dn = Turns("D_dn", 1, DEPTH)
        D_y = Turns("D_y", 1, DEPTH)
        D_out = Steps("D_out", 1, DEPTH, 16)
        E_y = Steps("E_y", 1, unit=16)
        E_t = Turns("E_t", 1)
        E_f = Turns("E_f", 1)
        E_out = Steps("E_out", 1, unit=16)

        g1, b1, g2, b2, tm1, cm1, tdec, tfirst, tm2, cm2 = (vecs[:, n:n + 1] for n in range(10))
        tg1, tb1, tg2, tb2, mA1, mA2, ed, eu, e_td, om1, om2, _ = (derived[:, n:n + 1] for n in range(12))
        SA, CA, GA, SB_, CB, GB = range(6)

        def batch(q, i):
            return 2 * i + q

        def earlier(step, eng, b, part):
            if not (isinstance(b, int) and b == 0):
                step.done(eng, b - 1, part)

        def slots(eng, stages):
            def slot(s):
                for group, stage in stages:
                    if not isinstance(s, int) or 0 <= s - group < NB:
                        stage(s - group)

            for s in range(LAG):
                slot(s)
            with eng.Fori(LAG, NB) as s:
                slot(s)
            for s in range(NB, NB + LAG):
                slot(s)

        def span(b, n):
            return bass.ds(b * n, n)

        def blocks_of(eng, stages, drain=DRAIN):
            def step(q, i):
                for back, stage in stages:
                    j = DEPTH * i + q - back
                    if not isinstance(i, int) or 0 <= j < NBLK:
                        stage(j, (q - back) % DEPTH, i + (q - back) // DEPTH)

            for q in range(DEPTH):
                step(q, 0)
            with eng.Fori(1, NBLK // DEPTH) as i:
                for q in range(DEPTH):
                    step(q, i)
            for q in range(NBLK % DEPTH + drain):
                step(q, NBLK // DEPTH)

        block = ctx.enter_context(nc.Block())

        @block.sync
        def _(sp):
            def tokens(t, b):
                return t[b].rearrange("(j p) c -> p j c", p=P)

            def load(step, dst, src):
                step(sp.dma_start(dst, src))

            for s in (L_small, L_wmod, L_att, L_ffn, L_shared, L_experts, L_fill):
                s.begin(sp, 0, 0)
            load(L_small, vecs[:], ins["vecs"])
            load(L_small, cT[:], ins["cT"])
            A_x.begin(sp, 0)(sp.dma_start(xtok, tokens(ins["x"], 0)))
            load(L_wmod, up_experts[:, 0:2, :].rearrange("p a b -> p (a b)")[:, 0:6 * C], ins["wmod"])
            load(L_small, router[:], ins["routerT"])
            for w, n in ((Wk, "WkT"), (Wv, "WvT"), (Wr, "WrT"), (Wo, "WoT")):
                load(L_att, w[:], ins[n])
            load(L_ffn, Fk[:], ins["FkT"])
            load(L_ffn, Fv[:], ins["FvT"].rearrange("(k p) c -> p k c", p=P))
            load(L_ffn, Fr[:], ins["FrT"])
            A_xT.begin(sp, 0)(sp.dma_start(xT, ins["xT"][:, 0:T]))
            load(L_shared, Wg[:], ins["gateT"])
            load(L_shared, Wu[:], ins["upT"])
            load(L_shared, Wd[:], ins["downT"].rearrange("(k p) c -> p k c", p=P))
            load(L_shared, down_experts[:, 0], ins["down"][:, 0:P, :].rearrange("e p c -> p e c"))
            load(L_experts, down_experts[:, 1], ins["down"][:, P:2 * P, :].rearrange("e p c -> p e c"))
            K_rows.done(sp, 0, 0)
            load(L_experts, up_experts[:, 0:E // 2, :], ins["gate_up"][0:E // 2].rearrange("e p f -> p e f"))
            load(L_experts, up_experts[:, E // 2:, :], ins["gate_up"][E // 2:].rearrange("e p f -> p e f"))
            K_pool.done(sp, 0, 0)
            load(L_fill, sorted_rows.rearrange("(k p) r -> p k r", p=P),
                 pad_row[:].rearrange("p (o r) -> p o r", o=1).broadcast_to([P, NBLK, ROW]))
            def refill_x(b):
                A_n1.before(sp, b)
                A_x.begin(sp, b)(sp.dma_start(xtok, tokens(ins["x"], b)))

            def refill_xT(b):
                A_x3.before(sp, b)
                A_xT.begin(sp, b)(sp.dma_start(xT, ins["xT"][:, span(b, T)]))

            for b in range(1, LAG):
                refill_x(b)
            with sp.Fori(LAG, NB) as s:
                refill_x(s)
                refill_xT(s - LAG + 1)
            for b in range(NB - LAG + 1, NB):
                refill_xT(b)

            B_out.done(sp, 0, 0)

            def block_in(j, q, i):
                if not (isinstance(i, int) and i == 0):
                    D_act.done(sp, q, i - 1)
                D_x.begin(sp, q, i)(sp.dma_start(xb[q], sorted_rows[span(j, P), :]))

            blocks_of(sp, [(0, block_in)], 0)

            for q in range(DEPTH):
                D_out.done(sp, q, (NBLK - 1 - q) // DEPTH)
            for q in range(2):
                E_y.begin(sp, q, 0)(sp.dma_start(yt[q], y_rows[q * T:(q + 1) * T, :].rearrange("(j p) c -> p j c", p=P)))
            with sp.Fori(1, PAIRS) as i:
                for q in range(2):
                    E_t.before(sp, q, i)
                    E_y.begin(sp, q, i)(sp.dma_start(yt[q], y_rows[span(batch(q, i), T), :].rearrange("(j p) c -> p j c", p=P)))

        @block.gpsimd
        def _(pool):
            K = K_pool.begin(pool, 0, 0)
            gpsimd[0] = pool
            for s in lifts["pool"]:
                s.lift(pool)
            K(pool.memset(ident[:], 0.0))
            K(pool.memset(neghalf[:], -0.5), True)
            K(pool.affine_select(out=ident[:], in_=ident[:], compare_op=ALU.not_equal, fill=1.0, base=0,
                                 pattern=[[-1, P]], channel_multiplier=1))
            K(pool.memset(ones_bf[:], 1.0), True)
            K(pool.affine_select(out=before_bf[:], in_=ones_bf[:], compare_op=ALU.is_gt, fill=0.0, base=0,
                                 pattern=[[1, P]], channel_multiplier=-1))
            K(pool.memset(pad_row[:, 0:C], 0.0))
            K(pool.memset(pad_row[:, C:ROW].bitcast(I32), NOROW))
            K(pool.iota(rows[:, :, C:C + 1].bitcast(I32), pattern=[[P, NTT], [1, 1]], base=0, channel_multiplier=1))
            K(pool.memset(rows[:, :, C + 1:ROW], 0.0))
            for t in (x1p, x2p):
                K(pool.memset(t[:, 0:1], 0.0))
                K(pool.memset(t[:, T + 1:T + 2], 0.0))
            for t in (apad, bpad):
                K(pool.memset(t[:, 0:1], 0.0))
            assert K.count == K.n
            K_rows.done(pool, 0, 0)

            def rs(n):
                def stage(b):
                    A_st[n].done(pool, b)
                    S = A_rs[n].begin(pool, b)
                    S(pool.tensor_scalar(rstd[n], mv[n][:, :, 1], EPS, None, ALU.add), True)
                    S(pool.tensor_tensor(rstd[n], rstd[n], neghalf[:], ALU.pow), n >= 2)
                    if n >= 2:
                        S(pool.tensor_scalar(shift[n - 2], mv[n][:, :, 0], -1.0, None, ALU.mult), True)
                        S(pool.tensor_tensor(shift[n - 2], shift[n - 2], rstd[n], ALU.mult))
                return stage

            def modulate(b):
                A_n1.done(pool, b)
                S = A_mod.begin(pool, b)
                row = lambda t: t[:, bass.ds(b, 1), :].broadcast_to([P, NT, C])
                S(pool.tensor_tensor(ht, ht, row(ca_rows), ALU.mult), True)
                S(pool.tensor_tensor(ht, ht, row(sa_rows), ALU.add))

            def squares(b):
                A_sqp.begin(pool, b)
                for c in range(1, HC, 2):
                    A_relu.done(pool, b, c + 1)
                    A_sqp(pool.tensor_tensor(relus[1], relus[1], relus[1], ALU.mult))

            slots(pool, [(2, rs(2)), (0, rs(0)), (0, modulate), (3, rs(3)), (2, squares), (0, rs(1))])

            A_rows.done(pool, NB - 1)
            S = B_pool.begin(pool, 0, 0)
            small_ints = dict(allow_small_or_imprecise_dtypes=True)
            S(pool.iota(iota_e, pattern=[[0, NTT], [-1, E]], base=E, channel_multiplier=0, **small_ints))
            S(pool.iota(iota_t, pattern=[[P, NTT]], base=0, channel_multiplier=0, **small_ints))
            S(pool.iota(iota_blk, pattern=[[1, NBLK], [0, E]], base=0, channel_multiplier=0, **small_ints))
            S(pool.memset(ones_e, 1.0))
            L_fill.done(pool, 0, 0)
            B_slot.done(pool, 0, 0, 16)
            S = B_out.begin(pool, 0, 0)
            for n in range(NTT):
                S(pool.indirect_dma_start(sorted_rows, bass.IndirectOffsetOnAxis(slot_i[:, n:n + 1], 0), rows[:, n, :], None))

            def block_out(j, q, i):
                D_y.done(pool, q, i)
                D_out.begin(pool, q, i)(pool.indirect_dma_start(
                    y_rows, bass.IndirectOffsetOnAxis(number[q], 0), yb[q], None,
                    bounds_check=NB * T - 1, oob_is_err=False))

            blocks_of(pool, [(0, block_out)], 0)

        @block.vector
        def _(dve):
            for s in lifts["dve"]:
                s.lift(dve)
            K = K_dve.begin(dve, 0, 0)
            L_small.done(dve, 0, 0)
            K_act.done(dve, 0, 0, 1)
            K(dve.tensor_scalar(sc[:], sc[:], 1.0, None, ALU.add), True)
            K(dve.reciprocal(sc[:], sc[:]), True)
            K(dve.tensor_tensor(sc[:], sc[:], cT[:], ALU.mult), True)
            scb = h2_all[:].rearrange("p (b c) -> p b c", c=T)[:, :, 0:P]
            K(dve.tensor_copy(scb, sc[:].rearrange("p (b o) -> p b o", o=1).broadcast_to([P, NB, P])))
            K_act.done(dve, 0, 0, 4)
            K(dve.tensor_scalar(om1, tm1, -1.0, 1.0, ALU.mult, ALU.add), True)
            K(dve.tensor_scalar(om2, tm2, -1.0, 1.0, ALU.mult, ALU.add), True)
            K(dve.tensor_copy(mA1, om1))
            K(dve.tensor_copy(mA2, om2), True)
            K(dve.tensor_tensor(mA1[0:HALF], om1[0:HALF], cm1[0:HALF], ALU.add))
            K(dve.tensor_tensor(mA2[0:HALF], om2[0:HALF], cm2[0:HALF], ALU.add))
            K(dve.tensor_tensor(tg1, tm1, g1, ALU.mult))
            K(dve.tensor_tensor(tb1, tm1, b1, ALU.mult))
            K(dve.tensor_tensor(tg2, tm2, g2, ALU.mult))
            K(dve.tensor_tensor(tb2, tm2, b2, ALU.mult))
            K(dve.memset(decay[:], 1.0), True)
            K(dve.tensor_scalar(decay[:], decay[:], ed, None, ALU.mult))
            K_pe.done(dve, 0, 0, 1)
            K(dve.tensor_copy(modc[:], bank[0][:, 0:6 * NB].rearrange("p (n b) -> p n b", b=NB)), True)
            for n in (CA, CB):
                K(dve.tensor_scalar(modc[:, n], modc[:, n], 1.0, None, ALU.add))
            for n, s in ((GA, small[:, 0:2 * NB]), (GB, small[:, 2 * NB:4 * NB])):
                sign, mag = s[:, 0:NB], s[:, NB:2 * NB]
                K(dve.tensor_scalar(sign, modc[:, n], 0.0, 2.0, ALU.is_ge, ALU.mult), True)
                K(dve.tensor_scalar(sign, sign, -1.0, None, ALU.add), True)
                K(dve.tensor_scalar(mag, modc[:, n], -1.0, None, ALU.mult), True)
                K(dve.tensor_tensor(mag, mag, modc[:, n], ALU.max), True)
                K(dve.tensor_scalar(mag, mag, 0.25, None, ALU.max), True)
                K(dve.tensor_tensor(modc[:, n], mag, sign, ALU.mult), True)
            L_att.done(dve, 0, 0)
            K(dve.tensor_scalar(Wo[:], Wo[:], 0.5, None, ALU.mult), True)
            assert K.count == K.n
            R = K_rows.begin(dve, 0, 0)
            for n in range(NB // 2):
                K_pe.done(dve, 0, 0, 2 + n)
                v = bank[1 + n][:].rearrange("p (b m c) -> p b m c", b=2, m=2)
                R(dve.tensor_copy(sa_rows[:, 2 * n:2 * n + 2, :], v[:, :, 0]))
                R(dve.tensor_scalar(ca_rows[:, 2 * n:2 * n + 2, :], v[:, :, 1], 1.0, None, ALU.add))
            R.done(dve, 0, 0)
            K_pool.done(dve, 0, 0)

            def stats(n, b, src):
                if n >= 2:
                    A_rs[n].before(dve, b)
                S = A_st[n].begin(dve, b)
                s6 = stat[n].rearrange("p (j s) -> p j s", s=6)
                for j in range(NT):
                    S(dve.bn_stats(s6[:, j], src[:, j]), j == NT - 1 and "alone")
                for j in range(NT):
                    S(dve.bn_aggr(mv[n][:, j], s6[:, j]))

            def normalise(step, n, b, src, dst):
                A_rs[n].done(dve, b)
                S = step.begin(dve, b)
                for j in range(NT):
                    S(dve.tensor_scalar(dst[:, j], src[:, j], mv[n][:, j, 0:1], rstd[n][:, j:j + 1],
                                        ALU.subtract, ALU.mult))

            def norm1_stats(b):
                A_x.done(dve, b)
                stats(0, b, xtok)

            def norm1(b):
                A_t1.before(dve, b)
                normalise(A_n1, 0, b, xtok, ht)

            def norm2_stats(b):
                A_mod.done(dve, b)
                stats(1, b, ht)

            def norm2(b):
                normalise(A_n2, 1, b, ht, ht)

            def mix(step, xmix, xp, mA, cm, b):
                S = step.begin(dve, b)
                S(dve.scalar_tensor_tensor(xmix, xp[:, 0:T], mA, xmix, ALU.mult, ALU.add), True)
                S(dve.scalar_tensor_tensor(xmix[HALF:], xp[HALF:, 2:T + 2], cm[HALF:], xmix[HALF:], ALU.mult, ALU.add))

            def mix1(b):
                A_x1.done(dve, b)
                mix(A_mix, xm, x1p, mA1, cm1, b)

            def mix2(b):
                A_x2.done(dve, b)
                mix(A_mix2, xm2, x2p, mA2, cm2, b)

            def clamp(b):
                A_kvr.done(dve, b, 1)
                A_cl.begin(dve, b)(dve.tensor_scalar(ek, bank[bK][:], KMAX, None, ALU.min))

            def wkv_scans(b):
                A_exp.done(dve, b)
                A_wo.before(dve, b)
                S = A_wkv.begin(dve, b)
                S(dve.tensor_tensor(kv, ek, bank[bV][:], ALU.mult))
                S(dve.tensor_tensor_scan(bpad[:, 1:T + 1], decay[:], ek, 0.0, ALU.mult, ALU.add), True)
                S(dve.tensor_tensor_scan(apad[:, 1:T + 1], decay[:], kv, 0.0, ALU.mult, ALU.add))
                S(dve.scalar_tensor_tensor(ek, ek, eu, bpad[:, 0:T], ALU.mult, ALU.add), True)
                S(dve.scalar_tensor_tensor(num, kv, eu, apad[:, 0:T], ALU.mult, ALU.add))

            def wkv_divide(b):
                S = A_wkv
                S(dve.reciprocal(ek, ek), True)
                S(dve.scalar_tensor_tensor(num, er, 1.0, num, ALU.add, ALU.mult), True)
                S(dve.tensor_tensor(num, num, ek, ALU.mult))

            def norm3_stats(b):
                A_wo.done(dve, b)
                stats(2, b, tok(bX2))

            def residual(b):
                A_th.done(dve, b)
                A_fv.done(dve, b)
                A_xT.done(dve, b)
                A_t3.before(dve, b)
                S = A_x3.begin(dve, b)
                S(dve.scalar_tensor_tensor(er2, er2, 1.0, bank[bFV][:], ALU.add, ALU.mult), True)
                S(dve.scalar_tensor_tensor(er2, er2, 0.5, x2p[:, 1:T + 1], ALU.mult, ALU.add), True)
                S(dve.scalar_tensor_tensor(x3w, er2, modc[:, GA, bass.ds(b, 1)], xT, ALU.mult, ALU.add), True)
                S(dve.tensor_copy(x3_all[:, span(b, T)], x3w))

            def norm4_stats(b):
                A_t3.done(dve, b)
                stats(3, b, tok(bT3))

            def top_logit(b):
                A_lg.done(dve, b)
                S = A_top.begin(dve, b)
                lg = bank[bLG][:, 0:NT * E].rearrange("p (j e) -> p j e", e=E)
                S(dve.tensor_copy(logits[:, span(b, NT), :], lg))
                S(dve.tensor_reduce(top[:, span(b, NT)], lg, AX.X, ALU.max))

            def scored_rows(b):
                A_es.done(dve, b)
                S = A_rows.begin(dve, b)
                S(dve.tensor_scalar(eexp, eexp, 1.0, None, ALU.add), True)
                S(dve.reciprocal(eexp, eexp), True)
                A_rt.done(dve, b)
                S(dve.tensor_tensor(rows[:, span(b, NT), 0:C], tok(bRT),
                                    eexp.rearrange("p (j o) -> p j o", o=1).broadcast_to([P, NT, C]), ALU.mult))

            slots(dve, [(2, norm3_stats), (0, norm1_stats), (1, mix1), (0, norm1), (3, residual), (1, clamp),
                        (3, norm4_stats), (2, mix2), (1, wkv_scans), (0, norm2_stats), (1, wkv_divide),
                        (3, top_logit), (0, norm2), (3, scored_rows)])

            B_pool.done(dve, 0, 0)
            A_top.done(dve, NB - 1)
            te = lambda t: t.rearrange("p (n e) -> p n e", e=E)
            et = lambda t: te(t).rearrange("p n e -> p e n")
            over = lambda t, n: t.rearrange("p (n o) -> p n o", o=1).broadcast_to([P, NTT, n])
            S = B_hot.begin(dve, 0, 0)
            S(dve.tensor_tensor(te(cand), logits[:], over(top[:], E), ALU.is_equal), True)
            S(dve.tensor_tensor(cand, cand, iota_e, ALU.mult), True)
            S(dve.tensor_reduce(best, te(cand), AX.X, ALU.max), True)
            S(dve.tensor_tensor(te(onehot), te(iota_e), over(best, E), ALU.is_equal), True)
            S(dve.tensor_copy(onehot_b, onehot))

            def shared_act(q, i):
                S = C_act.begin(dve, q, i)
                for c in range(FC):
                    C_sg.done(dve, q, i, c + 1)
                    C_gu.done(dve, q, i, FC + c + 1)
                    S(dve.tensor_tensor(sg[q][c], sg[q][c], bank[4 * q + FC + c][:], ALU.mult))

            def shared_base(q, i):
                b = batch(q, i)
                C_dn.done(dve, q, i)
                x3 = x3_all[:, span(b, T)]
                C_base.begin(dve, q, i)(dve.scalar_tensor_tensor(
                    x3, bank[4 * q][:], modc[:, GB, bass.ds(b, 1)], x3, ALU.mult, ALU.add))

            def shared_pair(i):
                for q in range(2):
                    shared_act(q, i)
                for q in range(2):
                    shared_base(q, i)

            S = B_slot.begin(dve, 0, 0)
            B_cnt.done(dve, 0, 0)
            S(dve.tensor_copy(rank, bank[4][:]))
            S(dve.tensor_copy(total.rearrange("p (e n) -> p e n", e=E), et(bank[5][:])))
            S(dve.memset(seg, 1.0), True)
            S(dve.memset(seg.rearrange("p (e n) -> p e n", e=E)[:, :, 0:1], 0.0), True)
            S(dve.tensor_tensor_scan(cum, seg, total, 0.0, ALU.mult, ALU.add), True)
            cum3 = cum.rearrange("p (e n) -> p e n", e=E)
            S(dve.tensor_tensor(blocks.rearrange("p (e n) -> p e n", e=E), cum3[:, :, NTT - 1:NTT].broadcast_to([P, E, NTT]),
                                iota_t.rearrange("p (o n) -> p o n", o=1).broadcast_to([P, E, NTT]), ALU.is_gt), True)
            S(dve.tensor_reduce(nblk, blocks.rearrange("p (e n) -> p e n", e=E), AX.X, ALU.add), True)
            S(dve.tensor_tensor_scan(bend, ones_e, nblk, 0.0, ALU.mult, ALU.add), True)
            S(dve.tensor_tensor(bstart, bend, nblk, ALU.subtract), True)
            S(dve.tensor_scalar(bstart, bstart, float(P), None, ALU.mult), True)
            S(dve.tensor_tensor(cum, cum, total, ALU.subtract), True)
            S(dve.tensor_tensor(te(rank), te(rank), cum3.rearrange("p e n -> p n e"), ALU.add), True)
            S(dve.tensor_tensor(te(rank), te(rank), bstart.rearrange("p (o e) -> p o e", o=1).broadcast_to([P, NTT, E]), ALU.add), True)
            S(dve.tensor_tensor(rank, rank, onehot, ALU.mult), True)
            S(dve.tensor_reduce(slot_f, te(rank), AX.X, ALU.add), True)
            S(dve.tensor_copy(slot_i[:], slot_f), True)
            shared_pair(0)
            S(dve.tensor_tensor(ltmp[0:1].rearrange("p (j e) -> p j e", e=E),
                                bend[0:1].rearrange("p (o e) -> p o e", o=1).broadcast_to([1, NBLK, E]),
                                iota_blk[0:1].rearrange("p (j e) -> p j e", e=E), ALU.is_le), True)
            S(dve.tensor_reduce(esum[0:1], ltmp[0:1].rearrange("p (j e) -> p j e", e=E), AX.X, ALU.add), True)
            S(dve.tensor_scalar(esum[0:1], esum[0:1], float(E - 1), None, ALU.min), True)
            S(dve.memset(block_expert[:, NBLK:], 0))
            S(dve.tensor_copy(block_expert[:, 0:NBLK], esum[0:1]), True)
            assert S.count == S.n

            with dve.Fori(1, PAIRS) as i:
                shared_pair(i)

            def expert_act(j, q, i):
                D_out.before(dve, q, i)
                S = D_act.begin(dve, q, i)
                D_sg.done(dve, q, i)
                S(dve.tensor_copy(number[q], xb[q][:, C:C + 1].bitcast(I32)))
                S(dve.tensor_tensor(acte[q % 2], sge[q % 2], bank[2 + q % 2][:, F:2 * F], ALU.mult))

            def expert_aT(j, q, i):
                D_at.done(dve, q, i)
                D_aT.begin(dve, q, i)(dve.tensor_copy(aT[q % 2], bank[4 + q % 2][:, 0:F]))

            blocks_of(dve, [(2, expert_aT), (1, expert_act)])

            def last_residual(q, i):
                b = batch(q, i)
                E_t.done(dve, q, i)
                E_out.before(dve, q, i)
                E_f.begin(dve, q, i)(dve.scalar_tensor_tensor(
                    fin[q], bank[q][:], modc[:, GB, bass.ds(b, 1)], x3_all[:, span(b, T)], ALU.mult, ALU.add))

            for q in range(2):
                last_residual(q, 0)
            with dve.Fori(1, PAIRS) as i:
                for q in range(2):
                    last_residual(q, i)

        @block.scalar
        def _(act):
            K = K_act.begin(act, 0, 0)
            L_small.done(act, 0, 0)
            K(act.activation(sc[:], cT[:], ACT.Exp, scale=-1.0))
            K(act.activation(e_td, tdec, ACT.Exp), True)
            K(act.activation(eu, tfirst, ACT.Exp))
            K(act.activation(ed, e_td, ACT.Exp, scale=-1.0))
            K(act.activation(small[:, 40:41], tfirst, ACT.Tanh))
            K_dve.done(act, 0, 0)
            K_pool.done(act, 0, 0)

            def affine(dst, src, scale, bias):
                return act.activation(dst, src, ACT.Identity, bias=bias, scale=scale)

            def x1(b):
                A_t1.done(act, b)
                A_wo.before(act, b)
                S = A_x1.begin(act, b)
                S(affine(x1p[:, 1:T + 1], bank[bT1][:], g1, b1))
                S(affine(xm, bank[bT1][:], tg1, tb1))

            def tanh_r(b):
                A_kvr.done(act, b)
                A_exp.begin(act, b)(act.activation(er, bank[bR][:], ACT.Tanh, scale=0.5))

            def exp_k(b):
                A_cl.done(act, b)
                A_exp(act.activation(ek, ek, ACT.Exp))

            def norm_rows(step, n, b, src, dst):
                A_rs[n].done(act, b)
                S = step.begin(act, b)
                for j in range(NT):
                    S(affine(dst[:, j * C:(j + 1) * C], src[:, j * C:(j + 1) * C], rstd[n][:, j:j + 1],
                             shift[n - 2][:, j:j + 1]))

            def norm3(b):
                norm_rows(A_n3, 2, b, bank[bX2], n3t)

            def norm4(b):
                norm_rows(A_n4, 3, b, bank[bT3], n4t)

            def x2(b):
                A_t2.done(act, b)
                earlier(A_x3, act, b, 2)
                S = A_x2.begin(act, b)
                S(affine(x2p[:, 1:T + 1], bank[bT2][:], g2, b2))
                S(affine(xm2, bank[bT2][:], tg2, tb2))

            def relu_chunks(b):
                A_fr.done(act, b)
                A_x3.before(act, b)
                A_th.begin(act, b)(act.activation(er2, bank[bFR][:], ACT.Tanh, scale=0.5))
                A_relu.begin(act, b)
                A_sqa.begin(act, b)
                for c in range(HC):
                    A_fk.done(act, b, c + 1)
                    if c >= 2:
                        A_fv.done(act, b, c - 1)
                    A_relu(act.activation(relus[c % 2], bank[(bFK, bFK2)[c % 2]][:], ACT.Relu), c % 2 == 0)
                    if c % 2 == 0:
                        A_sqa(act.activation(relus[0], relus[0], ACT.Square))

            def h2(b):
                A_t4.done(act, b)
                A_rt.before(act, b)
                S = A_h2.begin(act, b)
                s, t = modc[:, CB, bass.ds(b, 1)], modc[:, SB_, bass.ds(b, 1)]
                S(affine(h2w, bank[bT4][:], s, t))
                S(affine(h2_all[:, span(b, T)], bank[bT4][:], s, t))

            def exp_top(b):
                A_top.done(act, b)
                A_rows.before(act, b)
                A_es.begin(act, b)(act.activation(eexp, top[:, span(b, NT)], ACT.Exp, scale=-1.0))

            slots(act, [(2, norm3), (2, x2), (1, tanh_r), (1, exp_k), (3, norm4), (2, relu_chunks), (3, h2),
                        (3, exp_top), (0, x1)])

            def shared_silu(i):
                if isinstance(i, int):
                    A_rows.done(act, NB - 1)
                for q in range(2):
                    S = C_sg.begin(act, q, i)
                    C_dn.before(act, q, i)
                    for c in range(FC):
                        C_gu.done(act, q, i, c + 1)
                        S(act.activation(sg[q][c], bank[4 * q + c][:], ACT.Silu))

            shared_silu(0)
            with act.Fori(1, PAIRS) as i:
                shared_silu(i)

            def expert_xT(j, q, i):
                D_t.done(act, q, i)
                D_xT.begin(act, q, i)(act.copy(xbT[q % 2], bank[q % 2][:, 0:P]))

            def expert_silu(j, q, i):
                D_gu.done(act, q, i)
                D_sg.begin(act, q, i)(act.activation(sge[q % 2], bank[2 + q % 2][:, 0:F], ACT.Silu))

            def expert_y(j, q, i):
                D_dn.done(act, q, i)
                D_out.before(act, q, i)
                D_y.begin(act, q, i)(act.copy(yb[q], bank[6 + q % 2][:, 0:C]))

            blocks_of(act, [(0, expert_xT), (1, expert_silu), (3, expert_y)])

            for q in range(2):
                E_f.done(act, q, 0)
                E_out.begin(act, q, 0)(act.dma_start(out_t[:, q * T:(q + 1) * T], fin[q]))
            with act.Fori(1, PAIRS) as i:
                for q in range(2):
                    E_f.done(act, q, i)
                    E_out.begin(act, q, i)(act.dma_start(out_t[:, span(batch(q, i), T)], fin[q]))
            for q in range(2):
                E_out.done(act, q, PAIRS - 1)

        @block.tensor
        def _(pe):
            for s in lifts["pe"]:
                s.lift(pe)
            K_dve.done(pe, 0, 0, 4)
            L_wmod.done(pe, 0, 0)
            K = K_pe.begin(pe, 0, 0)
            wmod = up_experts[:, 0:2, :].rearrange("p a b -> p (a b)")[:, 0:6 * C]
            scb = h2_all[:].rearrange("p (b c) -> p b c", c=T)[:, :, 0:P]
            for n in range(6):
                last = pe.matmul(bank[0][:, n * NB:(n + 1) * NB], wmod[:, n * C:(n + 1) * C], sc[:], start=True, stop=True)
            K(last)
            for b in range(NB):
                last = pe.matmul(bank[1 + b // 2][:, b % 2 * 2 * C:(b % 2 + 1) * 2 * C], scb[:, b], wmod[:, 0:2 * C], start=True, stop=True)
                if b % 2:
                    K(last)
            K_pool.done(pe, 0, 0)
            K_rows.done(pe, 0, 0)
            K_dve.done(pe, 0, 0)
            for s in (L_att, L_ffn, L_small):
                s.done(pe, 0, 0)

            def turn(out, src, **kw):
                for j in range(NT):
                    last = pe.transpose(out[:, j * P:(j + 1) * P], src[:, j * P:(j + 1) * P], ident[:])
                return last

            def flat(t):
                return t.rearrange("p j c -> p (j c)")

            def mm(out, w, x, start=True, stop=True):
                return pe.matmul(out, w, x, start=start, stop=stop)

            def t1(b):
                A_n2.done(pe, b)
                A_t1.begin(pe, b)(turn(bank[bT1], flat(ht)))

            def key_value_gate(b):
                A_mix.done(pe, b)
                A_rows_top_free(b)
                S = A_kvr.begin(pe, b)
                for n, w in ((bK, Wk), (bV, Wv), (bR, Wr)):
                    S(mm(bank[n][:], w[:], xm))

            def A_rows_top_free(b):
                if not isinstance(b, int) or b >= 3:
                    A_rows.done(pe, b - 3)
                    A_top.done(pe, b - 3)

            def wo(b):
                A_wkv.done(pe, b)
                A_n3.before(pe, b)
                for j in range(NT):
                    o, c = bank[bX2][:, j * P:(j + 1) * P], slice(j * P, (j + 1) * P)
                    pe.matmul(o, x1p[:, 1 + j * P:1 + (j + 1) * P], ident[:], start=True, stop=False, is_transpose=True)
                    last = mm(o, num[:, c], Wo[:], start=False)
                A_wo.begin(pe, b)(last)

            def t2(b):
                A_n3.done(pe, b)
                earlier(A_x3, pe, b, 1)
                A_t2.begin(pe, b)(turn(bank[bT2], n3t))

            def channel_mix_a(b):
                A_mix2.done(pe, b)
                A_fr.begin(pe, b)(mm(bank[bFR][:], Fr[:], xm2))
                A_fk.begin(pe, b)
                A_fv.begin(pe, b)
                key(0, b)
                A_th.done(pe, b)
                key(1, b)
                value(0, b)

            def channel_mix_b(b):
                for c in range(2, HC):
                    A_relu.done(pe, b, c - 1)
                    key(c, b)
                    value(c - 1, b)
                value(HC - 1, b)

            def key(c, b):
                A_fk(mm(bank[(bFK, bFK2)[c % 2]][:], Fk[:, c * P:(c + 1) * P], xm2))

            def value(c, b):
                (A_sqa if c % 2 == 0 else A_sqp).done(pe, b, c // 2 + 1)
                A_fv(mm(bank[bFV][:], Fv[:, c], relus[c % 2], start=c == 0, stop=c == HC - 1))

            def t3(b):
                A_x3.done(pe, b, 3)
                A_x1.done(pe, min(b + 2, NB - 1) if isinstance(b, int) else b + 2)
                A_t3.begin(pe, b)(turn(bank[bT3], x3w))

            def t4(b):
                A_n4.done(pe, b)
                A_t4.begin(pe, b)(turn(bank[bT4], n4t))

            def route(b):
                A_h2.done(pe, b)
                for j in range(NT):
                    last = mm(bank[bLG][:, j * E:(j + 1) * E], h2w[:, j * P:(j + 1) * P], router[:])
                A_lg.begin(pe, b)(last)
                A_rt.begin(pe, b)(turn(bank[bRT], h2w))

            slots(pe, [(1, key_value_gate), (2, t2), (3, t3), (2, channel_mix_a), (3, t4), (2, channel_mix_b),
                       (3, route), (1, wo), (0, t1)])

            L_shared.done(pe, 0, 0)
            A_rows.done(pe, NB - 1)

            def shared_up(q, i):
                C_base.before(pe, q, i)
                S = C_gu.begin(pe, q, i)
                h = h2_all[:, span(batch(q, i), T)]
                for n, w in enumerate((Wg, Wu)):
                    for c in range(FC):
                        S(mm(bank[4 * q + n * FC + c][:], w[:, c * P:(c + 1) * P], h))

            def shared_down(q, i):
                C_act.done(pe, q, i)
                for c in range(FC):
                    last = mm(bank[4 * q][:], Wd[:, c], sg[q][c], start=c == 0, stop=c == FC - 1)
                C_dn.begin(pe, q, i)(last)

            def shared_pair(i):
                for q in range(2):
                    shared_up(q, i)
                for q in range(2):
                    shared_down(q, i)

            shared_up(0, 0)
            B_hot.done(pe, 0, 0)
            S = B_cnt.begin(pe, 0, 0)
            S(mm(bank[4][:], before_bf[:], onehot_b))
            S(mm(bank[5][:], ones_bf[:], onehot_b))
            B_slot.done(pe, 0, 0, 2)
            shared_up(1, 0)
            for q in range(2):
                shared_down(q, 0)
            with pe.Fori(1, PAIRS) as i:
                shared_pair(i)
            L_experts.done(pe, 0, 0)
            B_slot.done(pe, 0, 0)

            def row_in(j, q, i):
                D_x.done(pe, q, i)
                D_t.begin(pe, q, i)(pe.transpose(bank[q % 2][:, 0:P], xb[q][:, 0:P], ident[:]))

            def expert_of(j):
                return pe.value_load(block_expert[0:1, bass.ds(j, 1)], min_val=0, max_val=E - 1)

            def gate_up(j, q, i):
                e = expert_of(j)
                D_xT.done(pe, q, i)
                D_gu.begin(pe, q, i)(mm(bank[2 + q % 2][:], xbT[q % 2], up_experts[:, bass.ds(e, 1), :].rearrange("p o f -> p (o f)")))

            def turn_act(j, q, i):
                D_act.done(pe, q, i)
                for c in range(FC):
                    last = pe.transpose(bank[4 + q % 2][:, c * P:(c + 1) * P], acte[q % 2][:, c * P:(c + 1) * P], ident[:])
                D_at.begin(pe, q, i)(last)

            def down(j, q, i):
                e = expert_of(j)
                D_aT.done(pe, q, i)
                if not isinstance(j, int) or j >= 2:
                    D_y.done(pe, (q - 2) % DEPTH, i + (q - 2) // DEPTH)
                for c in range(FC):
                    last = mm(bank[6 + q % 2][:, 0:C], aT[q % 2][:, c * P:(c + 1) * P],
                              down_experts[:, c, bass.ds(e, 1), :].rearrange("p o f -> p (o f)"), start=c == 0, stop=c == FC - 1)
                D_dn.begin(pe, q, i)(last)

            for q in range(2):
                C_base.done(pe, q, PAIRS - 1)
            blocks_of(pe, [(0, row_in), (1, gate_up), (2, turn_act), (3, down)])

            with pe.Fori(0, PAIRS) as i:
                for q in range(2):
                    E_y.done(pe, q, i)
                    E_f.before(pe, q, i)
                    E_t.begin(pe, q, i)(turn(bank[q], flat(yt[q])))


def kernel(**inputs):
    import concourse.bacc as bacc
    from concourse import mybir
    from concourse.bass_utils import run_bass_kernel_spmd

    def t(name):
        return np.ascontiguousarray(np.asarray(inputs[name]).T)

    x = np.ascontiguousarray(inputs["L0_attn_x"])
    nb, nt, c = x.shape
    vecs = ["L0_attn_ln1_g", "L0_attn_ln1_b", "L0_attn_ln2_g", "L0_attn_ln2_b", "L0_attn_att_time_mix",
            "L0_attn_att_combined_mix", "L0_attn_time_decay", "L0_attn_time_first", "L0_attn_ffn_time_mix",
            "L0_attn_ffn_combined_mix"]
    arrays = {
        "x": x,
        "xT": np.ascontiguousarray(x.reshape(nb * nt, c).T),
        "vecs": np.ascontiguousarray(np.stack([np.asarray(inputs[n]).reshape(c) for n in vecs], axis=1)),
        "cT": t("L0_c"),
        "wmod": np.ascontiguousarray(inputs["L0_wmod"]),
        "WkT": t("L0_attn_Wk"), "WvT": t("L0_attn_Wv"), "WrT": t("L0_attn_Wr"), "WoT": t("L0_attn_Wo"),
        "FkT": t("L0_attn_Fk"), "FvT": t("L0_attn_Fv"), "FrT": t("L0_attn_Fr"),
        "routerT": t("L0_ffn_w_router"),
        "gateT": t("L0_ffn_w_gate"), "upT": t("L0_ffn_w_up"), "downT": t("L0_ffn_w_down"),
        "gate_up": np.ascontiguousarray(inputs["L0_ffn_gate_up_proj"]),
        "down": np.ascontiguousarray(inputs["L0_ffn_down_proj"]),
    }
    nc = bacc.Bacc("TRN2", target_bir_lowering=False, num_devices=1)
    ins = {n: nc.dram_tensor(f"in_{n}", a.shape, mybir.dt.float32, kind="ExternalInput").ap() for n, a in arrays.items()}
    out_t = nc.dram_tensor("out_t", (c, nb * nt), mybir.dt.float32, kind="ExternalOutput").ap()
    program(nc, ins, out_t)
    got = run_bass_kernel_spmd(nc, [{f"in_{n}": a for n, a in arrays.items()}], core_ids=[0])
    return np.ascontiguousarray(got.results[0]["out_t"].T).reshape(nb, nt, c)
```

```python
import numpy as np


def program(nc, ins, out_t):
    import contextlib
    import concourse.bass as bass
    from concourse import mybir

    F32, I32, BF16 = mybir.dt.float32, mybir.dt.int32, mybir.dt.bfloat16
    ALU, ACT, AX = mybir.AluOpType, mybir.ActivationFunctionType, mybir.AxisListType

    NB, T, C = ins["x"].shape
    P = 128
    NT = T // P
    NTT = NB * NT
    PAIRS = NB // 2
    H = ins["FkT"].shape[1]
    HC = H // P
    CHUNKS = (0, 2, 1, 3)
    E = ins["routerT"].shape[1]
    F = ins["gateT"].shape[1]
    FC = F // P
    NBLK = NTT + E - 1
    ROW = C + 4
    NOROW = NB * T
    LAG = 3
    DEPTH = 6
    ENDS = 4
    DRAIN = 3
    EPS, KMAX = 1e-5, 60.0
    HALF = C // 2

    ctx = contextlib.ExitStack()
    with ctx:
        def sb(name, shape, dt=F32):
            return ctx.enter_context(nc.sbuf_tensor(name, shape, dt))

        ident = sb("ident", [P, P])
        identb = sb("ident_bf", [P, P], BF16)
        ones_bf = sb("ones_bf", [P, P], BF16)
        before_bf = sb("before_bf", [P, P], BF16)
        vecs = sb("vecs", [P, 10])
        derived = sb("derived", [P, 12])
        modc = sb("modc", [P, 6, NB])
        small = sb("small", [P, 48])
        cT = sb("cT", [P, NB])
        sc = sb("sc", [P, NB])
        ca_rows = sb("ca_rows", [P, NB, C])
        sa_rows = sb("sa_rows", [P, NB, C])
        decay = sb("decay", [P, T])
        Wk = sb("Wk", [P, C]); Wv = sb("Wv", [P, C]); Wr = sb("Wr", [P, C]); Wo = sb("Wo", [P, C])
        Fk = sb("Fk", [P, H]); Fv = sb("Fv", [P, HC, C]); Fr = sb("Fr", [P, C])
        Wg = sb("Wg", [P, F]); Wu = sb("Wu", [P, F]); Wd = sb("Wd", [P, FC, C])
        router = sb("router", [P, E])
        h2_all = sb("h2_all", [P, NB * T])
        x3_all = sb("x3_all", [P, NB * T])
        rows = sb("rows", [P, NTT, ROW])
        logits = sb("logits", [P, NTT, E])
        top = sb("top", [P, NTT])
        slot_i = sb("slot_i", [P, NTT], I32)
        block_expert = sb("block_expert", [1, NBLK + 1], I32)
        up_experts = sb("up_experts", [P, E, 2 * F])
        down_experts = sb("down_experts", [P, FC, E, C])

        WORK = 27 * (T + 8)
        work = sb("work", [P, WORK])
        at = [0]

        def carve(n):
            a = at[0]
            at[0] += n
            assert at[0] <= WORK, (at[0], WORK)
            return work[:, a:a + n]

        def two(n):
            return [carve(n), carve(n)]

        def tiles(ap):
            return ap.rearrange("p (j c) -> p j c", c=C)

        xtok, ht = tiles(carve(T)), tiles(carve(T))
        xT, xm, xm2 = carve(T), carve(T), carve(T)
        x1p, x2p = carve(T + 2), carve(T + 2)
        ek, er, kv, num, er2 = carve(T), carve(T), carve(T), carve(T), carve(T)
        apad, bpad = carve(T + 1), carve(T + 1)
        n3t, n4t = carve(T), carve(T)
        relus = [carve(T) for _ in range(HC)]
        h2w, x3w = carve(T), carve(T)
        stat = [carve(6 * NT) for _ in range(4)]
        mv = [carve(2 * NT).rearrange("p (j s) -> p j s", s=2) for _ in range(4)]
        rstd = [carve(NT) for _ in range(4)]
        shift = [carve(NT) for _ in range(2)]
        eexp = carve(NT)
        neghalf = sb("neghalf", [P, NT])

        at[0] = 0
        G = NTT * E
        onehot = carve(G); rank = carve(G); total = carve(G); cum = carve(G); seg = carve(G); cand = carve(G)
        onehot_b = carve(G // 2).bitcast(BF16)
        blocks = carve(E * NTT); bend = carve(E); nblk = carve(E); bstart = carve(E); best = carve(NTT); slot_f = carve(NTT)
        ltmp = carve(NBLK * E); esum = carve(NBLK)
        iota_e = sb("iota_e", [P, G])[:]; iota_t = sb("iota_t", [P, NTT])[:]
        iota_blk = sb("iota_blk", [P, NBLK * E])[:]; ones_e = sb("ones_e", [P, E])[:]
        sg = [[carve(T) for _ in range(FC)] for _ in range(2)]
        xb = [carve(ROW) for _ in range(DEPTH)]
        xbT = two(P)
        sge, acte, aT = two(F), two(F), two(F)
        yb = [carve(C) for _ in range(DEPTH)]
        number = [carve(1).bitcast(I32) for _ in range(DEPTH)]
        at[0] = 0
        yt = [tiles(carve(T)) for _ in range(ENDS)]; fin = [carve(T) for _ in range(ENDS)]
        pad_row = sb("pad_row", [P, ROW])

        bank = [ctx.enter_context(nc.psum_tensor(f"bank{n}", [P, 512], F32)) for n in range(8)]
        bR, bK, bV, bT2, bX2, bT3, bFK, bFK2 = range(8)
        bFV, bLG, bT1, bFR, bT4, bRT = bR, bK, bV, bT2, bX2, bT3
        tok = lambda n: bank[n][:].rearrange("p (j c) -> p j c", c=C)
        sorted_rows = nc.dram_tensor("sorted_rows", [NBLK * P, ROW], F32, kind="Internal").ap()
        y_rows = nc.dram_tensor("y_rows", [NB * T, C], F32, kind="Internal").ap()

        lone_waits = [ctx.enter_context(nc.semaphore(f"lone_waits{n}")) for n in range(2)]
        gpsimd = [None]
        def wait(eng, semaphore, value, alone=False):
            w = eng.wait_ge(semaphore, value)
            if not isinstance(value, int):
                if eng is gpsimd[0]:
                    w.then_inc(lone_waits[0], 1)
                elif alone:
                    w.then_inc(lone_waits[1], 1)

        class Steps:

            def __init__(self, name, n, slots=2, unit=1):
                self.n, self.unit = n * unit, unit
                self.sem = [ctx.enter_context(nc.semaphore(f"{name}{q}")) for q in range(slots)]
                self.count = 0

            def start(self, q, i):
                return i * self.n

            def at(self, q):
                return self.sem[q]

            def begin(self, eng, q, i):
                self.eng, self.q, self.i, self.count = eng, q, i, 0
                return self

            def __call__(self, instruction, then_wait=False):
                self.count += self.unit
                assert self.count <= self.n
                instruction.then_inc(self.at(self.q), self.unit)
                if then_wait:
                    wait(self.eng, self.at(self.q), self.start(self.q, self.i) + self.count, then_wait == "alone")

            def done(self, eng, q, i, part=None):
                wait(eng, self.at(q), self.start(q, i) + (self.n if part is None else part * self.unit))

            def before(self, eng, q, i):
                if not (isinstance(i, int) and i == 0):
                    wait(eng, self.at(q), self.start(0, i))

        class Turns(Steps):

            def __init__(self, name, n, places=2):
                super().__init__(name, n, 1)
                self.places = places

            def start(self, q, i):
                return (self.places * i + q) * self.n

            def at(self, q):
                return self.sem[0]

            def before(self, eng, q, i):
                if not (isinstance(i, int) and i == 0):
                    self.done(eng, q, i - 1)

        class Line(Steps):

            def __init__(self, name, n, unit=1):
                super().__init__(name, n, 1, unit)

            def begin(self, eng, b):
                return super().begin(eng, 0, b)

            def done(self, eng, b, part=None):
                super().done(eng, 0, b, part)

            def before(self, eng, b):
                super().before(eng, 0, b)

        def once(name, n, unit=1):
            return Steps(name, n, 1, unit)

        L_small = once("L_small", 2, 16)
        L_wmod = once("L_wmod", 1, 16)
        L_att = once("L_att", 5, 16)
        L_ffn = once("L_ffn", 3, 16)
        L_shared = once("L_shared", 4, 16)
        L_experts = once("L_experts", 3, 16)
        L_fill = once("L_fill", 1, 16)
        K_pool = once("K_pool", 15)
        K_dve = once("K_dve", 32)
        K_act = once("K_act", 5)
        K_pe = once("K_pe", 1 + NB // 2)
        K_rows = once("K_rows", NB // 2 * 2)
        A_x = Line("A_x", 1, unit=16)
        A_xT = Line("A_xT", 1, unit=16)
        A_st = [Line(f"A_st{n}_", 2 * NT) for n in range(4)]
        A_rs = [Line(f"A_rs{n}_", 2 if n < 2 else 4) for n in range(4)]
        A_n1 = Line("A_n1", NT)
        A_mod = Line("A_mod", 2)
        A_n2 = Line("A_n2", NT)
        A_t1 = Line("A_t1", 1)
        A_x1 = Line("A_x1", 2)
        A_mix = Line("A_mix", 2)
        A_kv = Line("A_kv", 2)
        A_r = Line("A_r", 1)
        A_tanh = Line("A_tanh", 1)
        A_exp = Line("A_exp", 1)
        A_wkv = Line("A_wkv", 8)
        A_cl = Line("A_cl", 1)
        A_wo = Line("A_wo", 1)
        A_n3 = Line("A_n3", NT)
        A_t2 = Line("A_t2", 1)
        A_x2 = Line("A_x2", 2)
        A_mix2 = Line("A_mix2", 2)
        A_fr = Line("A_fr", 1)
        A_fk = Line("A_fk", HC)
        A_relu = Line("A_relu", HC)
        A_sqa = Line("A_sqa", HC // 2)
        A_sqp = Line("A_sqp", HC // 2)
        A_fv = Line("A_fv", HC)
        A_th = Line("A_th", 1)
        A_x3 = Line("A_x3", 3)
        A_keep = Line("A_keep", 1)
        A_t3 = Line("A_t3", 1)
        A_n4 = Line("A_n4", NT)
        A_t4 = Line("A_t4", 1)
        A_h2 = Line("A_h2", 2)
        A_lg = Line("A_lg", 1)
        A_rt = Line("A_rt", 1)
        A_top = Line("A_top", 2)
        A_es = Line("A_es", 1)
        A_rows = Line("A_rows", 3)
        B_hot = once("B_hot", 5)
        B_cnt = once("B_cnt", 2)
        B_slot = once("B_slot", 21)
        B_pool = once("B_pool", 4)
        B_out = once("B_out", NTT, 16)
        C_gu = Turns("C_gu", 2 * FC)
        C_sg = Turns("C_sg", FC)
        C_act = Turns("C_act", FC)
        C_dn = Turns("C_dn", 1)
        C_base = Turns("C_base", 1)
        D_x = Steps("D_x", 1, DEPTH, 16)
        D_t = Turns("D_t", 1, DEPTH)
        D_xT = Turns("D_xT", 1, DEPTH)
        D_gu = Turns("D_gu", 1, DEPTH)
        D_sg = Turns("D_sg", 1, DEPTH)
        D_act = Turns("D_act", 2, DEPTH)
        D_at = Turns("D_at", 1, DEPTH)
        D_aT = Turns("D_aT", 1, DEPTH)
        D_dn = Turns("D_dn", 1, DEPTH)
        D_y = Turns("D_y", 1, DEPTH)
        D_out = Steps("D_out", 1, DEPTH, 16)
        E_y = Steps("E_y", 1, ENDS, unit=16)
        E_t = Turns("E_t", 1, ENDS)
        E_f = Turns("E_f", 1, ENDS)
        E_out = Steps("E_out", 1, ENDS, unit=16)

        g1, b1, g2, b2, tm1, cm1, tdec, tfirst, tm2, cm2 = (vecs[:, n:n + 1] for n in range(10))
        tg1, tb1, tg2, tb2, mA1, mA2, ed, eu, e_td, om1, om2, _ = (derived[:, n:n + 1] for n in range(12))
        SA, CA, GA, SB_, CB, GB = range(6)

        def batch(q, i):
            return 2 * i + q

        def slots(eng, stages):
            def slot(s):
                for group, stage in stages:
                    if not isinstance(s, int) or 0 <= s - group < NB:
                        stage(s - group)

            for s in range(LAG):
                slot(s)
            with eng.Fori(LAG, NB) as s:
                slot(s)
            for s in range(NB, NB + LAG):
                slot(s)

        def last_batches(eng, stage):
            for q in range(ENDS):
                stage(q, q, 0)
            with eng.Fori(1, NB // ENDS) as i:
                for q in range(ENDS):
                    stage(ENDS * i + q, q, i)

        def span(b, n):
            return bass.ds(b * n, n)

        def blocks_of(eng, stages, drain=DRAIN):
            def step(q, i):
                for back, stage in stages:
                    j = DEPTH * i + q - back
                    if not isinstance(i, int) or 0 <= j < NBLK:
                        stage(j, (q - back) % DEPTH, i + (q - back) // DEPTH, q < back)

            for q in range(DEPTH):
                step(q, 0)
            with eng.Fori(1, NBLK // DEPTH) as i:
                for q in range(DEPTH):
                    step(q, i)
            for q in range(NBLK % DEPTH + drain):
                step(q, NBLK // DEPTH)

        block = ctx.enter_context(nc.Block())

        @block.sync
        def _(sp):
            def tokens(t, b):
                return t[b].rearrange("(j p) c -> p j c", p=P)

            def load(step, dst, src):
                step(sp.dma_start(dst, src))

            for s in (L_small, L_wmod, L_att, L_ffn, L_shared, L_experts, L_fill):
                s.begin(sp, 0, 0)
            load(L_small, cT[:], ins["cT"])
            load(L_small, vecs[:], ins["vecs"])
            load(L_wmod, up_experts[:, 0:2, :].rearrange("p a b -> p (a b)")[:, 0:6 * C], ins["wmod"])
            A_x.begin(sp, 0)(sp.dma_start(xtok, tokens(ins["x"], 0)))
            for w, n in ((Wk, "WkT"), (Wv, "WvT"), (Wr, "WrT"), (Wo, "WoT")):
                load(L_att, w[:], ins[n])
            load(L_att, router[:], ins["routerT"])
            load(L_ffn, Fk[:], ins["FkT"])
            load(L_ffn, Fv[:], ins["FvT"].rearrange("(k p) c -> p k c", p=P))
            load(L_ffn, Fr[:], ins["FrT"])
            A_xT.begin(sp, 0)(sp.dma_start(xT, ins["xT"][:, 0:T]))

            def refill_x(b):
                A_n1.before(sp, b)
                A_x.begin(sp, b)(sp.dma_start(xtok, tokens(ins["x"], b)))

            def refill_xT(b):
                A_x3.before(sp, b)
                A_xT.begin(sp, b)(sp.dma_start(xT, ins["xT"][:, span(b, T)]))

            refill_x(1)
            load(L_shared, Wg[:], ins["gateT"])
            load(L_shared, Wu[:], ins["upT"])
            load(L_shared, Wd[:], ins["downT"].rearrange("(k p) c -> p k c", p=P))
            load(L_shared, down_experts[:, 0], ins["down"][:, 0:P, :].rearrange("e p c -> p e c"))
            load(L_experts, down_experts[:, 1], ins["down"][:, P:2 * P, :].rearrange("e p c -> p e c"))
            refill_x(2)
            K_rows.done(sp, 0, 0)
            load(L_experts, up_experts[:, 0:E // 2, :], ins["gate_up"][0:E // 2].rearrange("e p f -> p e f"))
            load(L_experts, up_experts[:, E // 2:, :], ins["gate_up"][E // 2:].rearrange("e p f -> p e f"))
            with sp.Fori(LAG, NB) as s:
                refill_x(s)
                refill_xT(s - LAG + 1)
            K_pool.done(sp, 0, 0)
            load(L_fill, sorted_rows.rearrange("(k p) r -> p k r", p=P),
                 pad_row[:].rearrange("p (o r) -> p o r", o=1).broadcast_to([P, NBLK, ROW]))
            for b in range(NB - LAG + 1, NB):
                refill_xT(b)

            B_out.done(sp, 0, 0)

            def block_in(j, q, i, old):
                if not (isinstance(i, int) and i == 0):
                    D_act.done(sp, q, i - 1)
                D_x.begin(sp, q, i)(sp.dma_start(xb[q], sorted_rows[span(j, P), :]))

            blocks_of(sp, [(0, block_in)], 0)

            for q in range(DEPTH):
                D_out.done(sp, q, (NBLK - 1 - q) // DEPTH)
            def y_in(b, q, i):
                E_t.before(sp, q, i)
                E_y.begin(sp, q, i)(sp.dma_start(yt[q], y_rows[span(b, T), :].rearrange("(j p) c -> p j c", p=P)))

            last_batches(sp, y_in)

        @block.gpsimd
        def _(pool):
            K = K_pool.begin(pool, 0, 0)
            gpsimd[0] = pool
            K(pool.memset(ident[:], 0.0))
            K(pool.memset(neghalf[:], -0.5), True)
            K(pool.affine_select(out=ident[:], in_=ident[:], compare_op=ALU.not_equal, fill=1.0, base=0,
                                 pattern=[[-1, P]], channel_multiplier=1))
            K(pool.memset(ones_bf[:], 1.0), True)
            K(pool.affine_select(out=before_bf[:], in_=ones_bf[:], compare_op=ALU.is_gt, fill=0.0, base=0,
                                 pattern=[[1, P]], channel_multiplier=-1))
            K(pool.memset(pad_row[:, 0:C], 0.0))
            K(pool.memset(pad_row[:, C:ROW].bitcast(I32), NOROW))
            K(pool.iota(rows[:, :, C:C + 1].bitcast(I32), pattern=[[P, NTT], [1, 1]], base=0, channel_multiplier=1))
            K(pool.memset(rows[:, :, C + 1:ROW], 0.0))
            for t in (x1p, x2p):
                K(pool.memset(t[:, 0:1], 0.0))
                K(pool.memset(t[:, T + 1:T + 2], 0.0))
            for t in (apad, bpad):
                K(pool.memset(t[:, 0:1], 0.0))
            assert K.count == K.n
            S = B_pool.begin(pool, 0, 0)
            small_ints = dict(allow_small_or_imprecise_dtypes=True)
            S(pool.iota(iota_e, pattern=[[0, NTT], [-1, E]], base=E, channel_multiplier=0, **small_ints))
            S(pool.iota(iota_t, pattern=[[P, NTT]], base=0, channel_multiplier=0, **small_ints))
            S(pool.iota(iota_blk, pattern=[[1, NBLK], [0, E]], base=0, channel_multiplier=0, **small_ints))
            S(pool.memset(ones_e, 1.0))

            def rs(n):
                def stage(b):
                    A_st[n].done(pool, b)
                    S = A_rs[n].begin(pool, b)
                    S(pool.tensor_scalar(rstd[n], mv[n][:, :, 1], EPS, None, ALU.add), True)
                    S(pool.tensor_tensor(rstd[n], rstd[n], neghalf[:], ALU.pow), n >= 2)
                    if n >= 2:
                        S(pool.tensor_scalar(shift[n - 2], mv[n][:, :, 0], -1.0, None, ALU.mult), True)
                        S(pool.tensor_tensor(shift[n - 2], shift[n - 2], rstd[n], ALU.mult))
                return stage

            def modulate(b):
                A_n1.done(pool, b)
                S = A_mod.begin(pool, b)
                row = lambda t: t[:, bass.ds(b, 1), :].broadcast_to([P, NT, C])
                S(pool.tensor_tensor(ht, ht, row(ca_rows), ALU.mult), True)
                S(pool.tensor_tensor(ht, ht, row(sa_rows), ALU.add))

            def square(c):
                def stage(b):
                    if c == 1:
                        A_sqp.begin(pool, b)
                    A_relu.done(pool, b, CHUNKS.index(c) + 1)
                    A_sqp(pool.tensor_tensor(relus[c], relus[c], relus[c], ALU.mult))
                return stage

            slots(pool, [(1, modulate), (3, square(1)), (1, rs(1)), (3, square(3)), (2, rs(2)), (0, rs(0)), (3, rs(3))])

            A_rows.done(pool, NB - 1)
            L_fill.done(pool, 0, 0)
            B_slot.done(pool, 0, 0, 16)
            S = B_out.begin(pool, 0, 0)
            for n in range(NTT):
                S(pool.indirect_dma_start(sorted_rows, bass.IndirectOffsetOnAxis(slot_i[:, n:n + 1], 0), rows[:, n, :], None))

            def block_out(j, q, i, old):
                D_y.done(pool, q, i)
                D_out.begin(pool, q, i)(pool.indirect_dma_start(
                    y_rows, bass.IndirectOffsetOnAxis(number[q], 0), yb[q], None,
                    bounds_check=NB * T - 1, oob_is_err=False))

            blocks_of(pool, [(0, block_out)], 0)

        @block.vector
        def _(dve):
            K = K_dve.begin(dve, 0, 0)
            L_small.done(dve, 0, 0)
            K_act.done(dve, 0, 0, 1)
            K(dve.tensor_scalar(sc[:], sc[:], 1.0, None, ALU.add), True)
            K(dve.reciprocal(sc[:], sc[:]), True)
            K(dve.tensor_tensor(sc[:], sc[:], cT[:], ALU.mult), True)
            scb = h2_all[:].rearrange("p (b c) -> p b c", c=T)[:, :, 0:P]
            K(dve.tensor_copy(scb, sc[:].rearrange("p (b o) -> p b o", o=1).broadcast_to([P, NB, P])))
            K_act.done(dve, 0, 0, 4)
            K(dve.tensor_scalar(om1, tm1, -1.0, 1.0, ALU.mult, ALU.add), True)
            K(dve.tensor_scalar(om2, tm2, -1.0, 1.0, ALU.mult, ALU.add), True)
            K(dve.tensor_copy(mA1, om1))
            K(dve.tensor_copy(mA2, om2), True)
            K(dve.tensor_tensor(mA1[0:HALF], om1[0:HALF], cm1[0:HALF], ALU.add))
            K(dve.tensor_tensor(mA2[0:HALF], om2[0:HALF], cm2[0:HALF], ALU.add))
            K(dve.tensor_tensor(tg1, tm1, g1, ALU.mult))
            K(dve.tensor_tensor(tb1, tm1, b1, ALU.mult))
            K(dve.tensor_tensor(tg2, tm2, g2, ALU.mult))
            K(dve.tensor_tensor(tb2, tm2, b2, ALU.mult))
            K(dve.memset(decay[:], 1.0), True)
            K(dve.tensor_scalar(decay[:], decay[:], ed, None, ALU.mult))
            K_pe.done(dve, 0, 0, 1)
            K(dve.tensor_copy(modc[:], bank[0][:, 0:6 * NB].rearrange("p (n b) -> p n b", b=NB)), True)
            for n in (CA, CB):
                K(dve.tensor_scalar(modc[:, n], modc[:, n], 1.0, None, ALU.add))
            for n, s in ((GA, small[:, 0:2 * NB]), (GB, small[:, 2 * NB:4 * NB])):
                sign, mag = s[:, 0:NB], s[:, NB:2 * NB]
                K(dve.tensor_scalar(sign, modc[:, n], 0.0, 2.0, ALU.is_ge, ALU.mult), True)
                K(dve.tensor_scalar(sign, sign, -1.0, None, ALU.add), True)
                K(dve.tensor_scalar(mag, modc[:, n], -1.0, None, ALU.mult), True)
                K(dve.tensor_tensor(mag, mag, modc[:, n], ALU.max), True)
                K(dve.tensor_scalar(mag, mag, 0.25, None, ALU.max), True)
                K(dve.tensor_tensor(modc[:, n], mag, sign, ALU.mult), True)
            L_att.done(dve, 0, 0)
            K(dve.tensor_scalar(Wo[:], Wo[:], 0.5, None, ALU.mult), True)
            assert K.count == K.n
            R = K_rows.begin(dve, 0, 0)
            for n in range(NB // 2):
                K_pe.done(dve, 0, 0, 2 + n)
                v = bank[1 + n][:].rearrange("p (b m c) -> p b m c", b=2, m=2)
                R(dve.tensor_copy(sa_rows[:, 2 * n:2 * n + 2, :], v[:, :, 0]))
                R(dve.tensor_scalar(ca_rows[:, 2 * n:2 * n + 2, :], v[:, :, 1], 1.0, None, ALU.add))
            R.done(dve, 0, 0)
            K_pool.done(dve, 0, 0)

            def stats(n, b, src):
                S = A_st[n].begin(dve, b)
                s6 = stat[n].rearrange("p (j s) -> p j s", s=6)
                for j in range(NT):
                    S(dve.bn_stats(s6[:, j], src[:, j]), j == NT - 1 and "alone")
                for j in range(NT):
                    S(dve.bn_aggr(mv[n][:, j], s6[:, j]))

            def normalise(step, n, b, src, dst):
                A_rs[n].done(dve, b)
                S = step.begin(dve, b)
                for j in range(NT):
                    S(dve.tensor_scalar(dst[:, j], src[:, j], mv[n][:, j, 0:1], rstd[n][:, j:j + 1],
                                        ALU.subtract, ALU.mult))

            def norm1_stats(b):
                A_x.done(dve, b)
                stats(0, b, xtok)

            def norm1(b):
                A_t1.before(dve, b)
                normalise(A_n1, 0, b, xtok, ht)

            def norm2_stats(b):
                A_mod.done(dve, b)
                stats(1, b, ht)

            def norm2(b):
                normalise(A_n2, 1, b, ht, ht)

            def mix(step, xmix, xp, mA, cm, b):
                S = step.begin(dve, b)
                S(dve.scalar_tensor_tensor(xmix, xp[:, 0:T], mA, xmix, ALU.mult, ALU.add), True)
                S(dve.scalar_tensor_tensor(xmix[HALF:], xp[HALF:, 2:T + 2], cm[HALF:], xmix[HALF:], ALU.mult, ALU.add))

            def mix1(b):
                A_x1.done(dve, b)
                mix(A_mix, xm, x1p, mA1, cm1, b)

            def mix2(b):
                A_x2.done(dve, b)
                mix(A_mix2, xm2, x2p, mA2, cm2, b)

            def clamp(b):
                A_kv.done(dve, b, 1)
                A_cl.begin(dve, b)(dve.tensor_scalar(ek, bank[bK][:], KMAX, None, ALU.min))

            def wkv_scans(b):
                A_exp.done(dve, b)
                A_kv.done(dve, b)
                S = A_wkv.begin(dve, b)
                S(dve.tensor_tensor(kv, ek, bank[bV][:], ALU.mult))
                S(dve.tensor_tensor_scan(bpad[:, 1:T + 1], decay[:], ek, 0.0, ALU.mult, ALU.add), True)
                S(dve.tensor_tensor_scan(apad[:, 1:T + 1], decay[:], kv, 0.0, ALU.mult, ALU.add))
                S(dve.scalar_tensor_tensor(ek, ek, eu, bpad[:, 0:T], ALU.mult, ALU.add), True)
                S(dve.scalar_tensor_tensor(num, kv, eu, apad[:, 0:T], ALU.mult, ALU.add))

            def wkv_divide(b):
                A_tanh.done(dve, b)
                S = A_wkv
                S(dve.reciprocal(ek, ek), True)
                S(dve.scalar_tensor_tensor(num, er, 1.0, num, ALU.add, ALU.mult), True)
                S(dve.tensor_tensor(num, num, ek, ALU.mult))

            def norm3_stats(b):
                A_wo.done(dve, b)
                stats(2, b, tok(bX2))

            def residual(b):
                A_th.done(dve, b)
                A_fv.done(dve, b)
                A_xT.done(dve, b)
                S = A_x3.begin(dve, b)
                S(dve.scalar_tensor_tensor(er2, er2, 1.0, bank[bFV][:], ALU.add, ALU.mult), True)
                S(dve.scalar_tensor_tensor(er2, er2, 0.5, x2p[:, 1:T + 1], ALU.mult, ALU.add), True)
                S(dve.scalar_tensor_tensor(x3w, er2, modc[:, GA, bass.ds(b, 1)], xT, ALU.mult, ALU.add))

            def norm4_stats(b):
                A_t3.done(dve, b)
                stats(3, b, tok(bT3))

            def top_logit(b):
                A_lg.done(dve, b)
                S = A_top.begin(dve, b)
                lg = bank[bLG][:, 0:NT * E].rearrange("p (j e) -> p j e", e=E)
                S(dve.tensor_copy(logits[:, span(b, NT), :], lg))
                S(dve.tensor_reduce(top[:, span(b, NT)], lg, AX.X, ALU.max))

            def scored_rows(b):
                A_es.done(dve, b)
                S = A_rows.begin(dve, b)
                S(dve.tensor_scalar(eexp, eexp, 1.0, None, ALU.add), True)
                S(dve.reciprocal(eexp, eexp), True)
                A_rt.done(dve, b)
                S(dve.tensor_tensor(rows[:, span(b, NT), 0:C], tok(bRT),
                                    eexp.rearrange("p (j o) -> p j o", o=1).broadcast_to([P, NT, C]), ALU.mult))

            slots(dve, [(2, norm3_stats), (0, norm1_stats), (3, residual), (1, mix1), (3, norm4_stats), (0, norm1),
                        (1, clamp), (2, mix2), (1, wkv_scans), (0, norm2_stats), (1, wkv_divide), (3, top_logit),
                        (0, norm2), (3, scored_rows)])

            B_pool.done(dve, 0, 0)
            A_top.done(dve, NB - 1)
            te = lambda t: t.rearrange("p (n e) -> p n e", e=E)
            et = lambda t: te(t).rearrange("p n e -> p e n")
            over = lambda t, n: t.rearrange("p (n o) -> p n o", o=1).broadcast_to([P, NTT, n])
            S = B_hot.begin(dve, 0, 0)
            S(dve.tensor_tensor(te(cand), logits[:], over(top[:], E), ALU.is_equal), True)
            S(dve.tensor_tensor(cand, cand, iota_e, ALU.mult), True)
            S(dve.tensor_reduce(best, te(cand), AX.X, ALU.max), True)
            S(dve.tensor_tensor(te(onehot), te(iota_e), over(best, E), ALU.is_equal), True)
            S(dve.tensor_copy(onehot_b, onehot))

            def shared_act(q, i):
                S = C_act.begin(dve, q, i)
                for c in range(FC):
                    C_sg.done(dve, q, i, c + 1)
                    C_gu.done(dve, q, i, FC + c + 1)
                    S(dve.tensor_tensor(sg[q][c], sg[q][c], bank[4 * q + FC + c][:], ALU.mult))

            def shared_base(q, i):
                b = batch(q, i)
                C_dn.done(dve, q, i)
                x3 = x3_all[:, span(b, T)]
                C_base.begin(dve, q, i)(dve.scalar_tensor_tensor(
                    x3, bank[4 * q][:], modc[:, GB, bass.ds(b, 1)], x3, ALU.mult, ALU.add))

            def shared_pair(i):
                for q in range(2):
                    shared_act(q, i)
                for q in range(2):
                    shared_base(q, i)

            shared_act(0, 0)
            S = B_slot.begin(dve, 0, 0)
            B_cnt.done(dve, 0, 0)
            S(dve.tensor_copy(rank, bank[4][:]))
            S(dve.tensor_copy(total.rearrange("p (e n) -> p e n", e=E), et(bank[5][:])))
            S(dve.memset(seg, 1.0), True)
            S(dve.memset(seg.rearrange("p (e n) -> p e n", e=E)[:, :, 0:1], 0.0), True)
            S(dve.tensor_tensor_scan(cum, seg, total, 0.0, ALU.mult, ALU.add), True)
            cum3 = cum.rearrange("p (e n) -> p e n", e=E)
            S(dve.tensor_tensor(blocks.rearrange("p (e n) -> p e n", e=E), cum3[:, :, NTT - 1:NTT].broadcast_to([P, E, NTT]),
                                iota_t.rearrange("p (o n) -> p o n", o=1).broadcast_to([P, E, NTT]), ALU.is_gt), True)
            S(dve.tensor_reduce(nblk, blocks.rearrange("p (e n) -> p e n", e=E), AX.X, ALU.add), True)
            S(dve.tensor_tensor_scan(bend, ones_e, nblk, 0.0, ALU.mult, ALU.add), True)
            S(dve.tensor_tensor(bstart, bend, nblk, ALU.subtract), True)
            S(dve.tensor_scalar(bstart, bstart, float(P), None, ALU.mult), True)
            S(dve.tensor_tensor(cum, cum, total, ALU.subtract), True)
            S(dve.tensor_tensor(te(rank), te(rank), cum3.rearrange("p e n -> p n e"), ALU.add), True)
            S(dve.tensor_tensor(te(rank), te(rank), bstart.rearrange("p (o e) -> p o e", o=1).broadcast_to([P, NTT, E]), ALU.add), True)
            S(dve.tensor_tensor(rank, rank, onehot, ALU.mult), True)
            S(dve.tensor_reduce(slot_f, te(rank), AX.X, ALU.add), True)
            S(dve.tensor_copy(slot_i[:], slot_f), True)
            shared_base(0, 0)
            shared_act(1, 0)
            shared_base(1, 0)
            S(dve.tensor_tensor(ltmp[0:1].rearrange("p (j e) -> p j e", e=E),
                                bend[0:1].rearrange("p (o e) -> p o e", o=1).broadcast_to([1, NBLK, E]),
                                iota_blk[0:1].rearrange("p (j e) -> p j e", e=E), ALU.is_le), True)
            S(dve.tensor_reduce(esum[0:1], ltmp[0:1].rearrange("p (j e) -> p j e", e=E), AX.X, ALU.add), True)
            S(dve.tensor_scalar(esum[0:1], esum[0:1], float(E - 1), None, ALU.min), True)
            S(dve.memset(block_expert[:, NBLK:], 0))
            S(dve.tensor_copy(block_expert[:, 0:NBLK], esum[0:1]), True)
            assert S.count == S.n

            with dve.Fori(1, PAIRS) as i:
                shared_pair(i)

            def expert_act(j, q, i, old):
                D_out.before(dve, q, i)
                S = D_act.begin(dve, q, i)
                D_sg.done(dve, q, i)
                S(dve.tensor_copy(number[q], xb[q][:, C:C + 1].bitcast(I32)))
                S(dve.tensor_tensor(acte[q % 2], sge[q % 2], bank[2 + q % 2][:, F:2 * F], ALU.mult))

            def expert_aT(j, q, i, old):
                D_at.done(dve, q, i)
                D_aT.begin(dve, q, i)(dve.tensor_copy(aT[q % 2], bank[4 + q % 2][:, 0:F]))

            blocks_of(dve, [(2, expert_aT), (1, expert_act)])

            def last_residual(b, q, i):
                E_t.done(dve, q, i)
                E_out.before(dve, q, i)
                E_f.begin(dve, q, i)(dve.scalar_tensor_tensor(
                    fin[q], bank[q][:], modc[:, GB, bass.ds(b, 1)], x3_all[:, span(b, T)], ALU.mult, ALU.add))

            last_batches(dve, last_residual)

        @block.scalar
        def _(act):
            K = K_act.begin(act, 0, 0)
            L_small.done(act, 0, 0)
            K(act.activation(sc[:], cT[:], ACT.Exp, scale=-1.0))
            K(act.activation(e_td, tdec, ACT.Exp), True)
            K(act.activation(eu, tfirst, ACT.Exp))
            K(act.activation(ed, e_td, ACT.Exp, scale=-1.0))
            K(act.activation(small[:, 40:41], tfirst, ACT.Tanh))
            K_dve.done(act, 0, 0)
            K_pool.done(act, 0, 0)

            def affine(dst, src, scale, bias):
                return act.activation(dst, src, ACT.Identity, bias=bias, scale=scale)

            def x1(b):
                A_t1.done(act, b)
                S = A_x1.begin(act, b)
                S(affine(x1p[:, 1:T + 1], bank[bT1][:], g1, b1))
                S(affine(xm, bank[bT1][:], tg1, tb1))

            def tanh_r(b):
                A_r.done(act, b)
                A_wkv.before(act, b)
                A_tanh.begin(act, b)(act.activation(er, bank[bR][:], ACT.Tanh, scale=0.5))

            def exp_k(b):
                A_cl.done(act, b)
                A_exp.begin(act, b)(act.activation(ek, ek, ACT.Exp))

            def norm_rows(step, n, b, src, dst):
                A_rs[n].done(act, b)
                S = step.begin(act, b)
                for j in range(NT):
                    S(affine(dst[:, j * C:(j + 1) * C], src[:, j * C:(j + 1) * C], rstd[n][:, j:j + 1],
                             shift[n - 2][:, j:j + 1]))

            def norm3(b):
                norm_rows(A_n3, 2, b, bank[bX2], n3t)

            def norm4(b):
                norm_rows(A_n4, 3, b, bank[bT3], n4t)

            def x2(b):
                A_t2.done(act, b)
                S = A_x2.begin(act, b)
                S(affine(x2p[:, 1:T + 1], bank[bT2][:], g2, b2))
                S(affine(xm2, bank[bT2][:], tg2, tb2))

            def tanh_r2(b):
                A_fr.done(act, b)
                A_th.begin(act, b)(act.activation(er2, bank[bFR][:], ACT.Tanh, scale=0.5))

            def relu(c):
                k = CHUNKS.index(c)

                def stage(b):
                    if k == 0:
                        A_relu.begin(act, b)
                    A_fk.done(act, b, k + 1)
                    A_relu(act.activation(relus[c], bank[(bFK, bFK2)[k % 2]][:], ACT.Relu))
                return stage

            def square(c):
                def stage(b):
                    if c == 0:
                        A_sqa.begin(act, b)
                    A_relu.done(act, b, CHUNKS.index(c) + 1)
                    A_sqa(act.activation(relus[c], relus[c], ACT.Square))
                return stage

            def keep_x3(b):
                A_x3.done(act, b)
                A_keep.begin(act, b)(act.copy(x3_all[:, span(b, T)], x3w))

            def h2(b):
                A_t4.done(act, b)
                S = A_h2.begin(act, b)
                s, t = modc[:, CB, bass.ds(b, 1)], modc[:, SB_, bass.ds(b, 1)]
                S(affine(h2w, bank[bT4][:], s, t))
                S(affine(h2_all[:, span(b, T)], bank[bT4][:], s, t))

            def exp_top(b):
                A_top.done(act, b)
                A_es.begin(act, b)(act.activation(eexp, top[:, span(b, NT)], ACT.Exp, scale=-1.0))

            slots(act, [(1, exp_k), (3, norm4), (1, tanh_r), (2, relu(0)), (2, square(0)), (3, keep_x3), (2, relu(2)),
                        (2, relu(1)), (2, relu(3)), (3, h2), (2, tanh_r2), (2, square(2)), (3, exp_top), (0, x1),
                        (1, norm3), (1, x2)])

            def shared_silu(i):
                if isinstance(i, int):
                    A_rows.done(act, NB - 1)
                for q in range(2):
                    S = C_sg.begin(act, q, i)
                    C_dn.before(act, q, i)
                    for c in range(FC):
                        C_gu.done(act, q, i, c + 1)
                        S(act.activation(sg[q][c], bank[4 * q + c][:], ACT.Silu))

            shared_silu(0)
            with act.Fori(1, PAIRS) as i:
                shared_silu(i)

            def expert_xT(j, q, i, old):
                D_t.done(act, q, i)
                D_xT.begin(act, q, i)(act.copy(xbT[q % 2], bank[q % 2][:, 0:P]))

            def expert_silu(j, q, i, old):
                D_gu.done(act, q, i)
                D_sg.begin(act, q, i)(act.activation(sge[q % 2], bank[2 + q % 2][:, 0:F], ACT.Silu))

            def expert_y(j, q, i, old):
                D_dn.done(act, q, i)
                D_out.before(act, q, i)
                D_y.begin(act, q, i)(act.copy(yb[q], bank[6 + q % 2][:, 0:C]))

            blocks_of(act, [(0, expert_xT), (1, expert_silu), (3, expert_y)])

            def store(b, q, i):
                E_f.done(act, q, i)
                E_out.begin(act, q, i)(act.dma_start(out_t[:, span(b, T)], fin[q]))

            last_batches(act, store)
            for q in range(ENDS):
                E_out.done(act, q, NB // ENDS - 1)

        @block.tensor
        def _(pe):
            K_dve.done(pe, 0, 0, 4)
            L_wmod.done(pe, 0, 0)
            K = K_pe.begin(pe, 0, 0)
            wmod = up_experts[:, 0:2, :].rearrange("p a b -> p (a b)")[:, 0:6 * C]
            scb = h2_all[:].rearrange("p (b c) -> p b c", c=T)[:, :, 0:P]
            for n in range(6):
                last = pe.matmul(bank[0][:, n * NB:(n + 1) * NB], wmod[:, n * C:(n + 1) * C], sc[:], start=True, stop=True)
            K(last)
            for b in range(NB):
                last = pe.matmul(bank[1 + b // 2][:, b % 2 * 2 * C:(b % 2 + 1) * 2 * C], scb[:, b], wmod[:, 0:2 * C], start=True, stop=True)
                if b % 2:
                    K(last)
            K_pool.done(pe, 0, 0)
            K_rows.done(pe, 0, 0)
            K_dve.done(pe, 0, 0)
            for s in (L_att, L_ffn, L_small):
                s.done(pe, 0, 0)

            def turn(out, src, **kw):
                for j in range(NT):
                    last = pe.transpose(out[:, j * P:(j + 1) * P], src[:, j * P:(j + 1) * P], ident[:])
                return last

            def flat(t):
                return t.rearrange("p j c -> p (j c)")

            def mm(out, w, x, start=True, stop=True):
                return pe.matmul(out, w, x, start=start, stop=stop)

            def t1(b):
                A_n2.done(pe, b)
                A_t1.begin(pe, b)(turn(bank[bT1], flat(ht)))

            def key1(b):
                A_mix.done(pe, b)
                A_kv.begin(pe, b)(mm(bank[bK][:], Wk[:], xm))

            def value1(b):
                A_kv(mm(bank[bV][:], Wv[:], xm))

            def gate1(b):
                A_r.begin(pe, b)(mm(bank[bR][:], Wr[:], xm))

            def wo(b):
                A_wkv.done(pe, b)
                for j in range(NT):
                    o, c = bank[bX2][:, j * P:(j + 1) * P], slice(j * P, (j + 1) * P)
                    pe.matmul(o, x1p[:, 1 + j * P:1 + (j + 1) * P], ident[:], start=True, stop=False, is_transpose=True)
                    last = mm(o, num[:, c], Wo[:], start=False)
                A_wo.begin(pe, b)(last)

            def t2(b):
                A_n3.done(pe, b)
                A_t2.begin(pe, b)(turn(bank[bT2], n3t))

            def keys2(b):
                A_mix2.done(pe, b)
                S = A_fk.begin(pe, b)
                for k, c in enumerate(CHUNKS):
                    if k >= 2:
                        A_relu.done(pe, b, k - 1)
                    S(mm(bank[(bFK, bFK2)[k % 2]][:], Fk[:, c * P:(c + 1) * P], xm2))

            def gate2(b):
                A_fr.begin(pe, b)(mm(bank[bFR][:], Fr[:], xm2))

            def values2(*chunks):
                def stage(b):
                    if chunks[0] == 0:
                        A_fv.begin(pe, b)
                    for c in chunks:
                        (A_sqa if c % 2 == 0 else A_sqp).done(pe, b, c // 2 + 1)
                        A_fv(mm(bank[bFV][:], Fv[:, c], relus[c], start=c == 0, stop=c == HC - 1))
                return stage

            def t3(b):
                A_x3.done(pe, b)
                A_t3.begin(pe, b)(turn(bank[bT3], x3w))

            def t4(b):
                A_n4.done(pe, b)
                A_t4.begin(pe, b)(turn(bank[bT4], n4t))

            def route(b):
                A_h2.done(pe, b)
                for j in range(NT):
                    last = mm(bank[bLG][:, j * E:(j + 1) * E], h2w[:, j * P:(j + 1) * P], router[:])
                A_lg.begin(pe, b)(last)

            def back(b):
                A_rt.begin(pe, b)(turn(bank[bRT], h2w))

            slots(pe, [(1, gate1), (2, keys2), (3, t4), (2, gate2), (2, values2(0, 1)), (3, route), (3, back), (1, wo),
                       (2, values2(2, 3)), (0, t1), (2, t3), (1, t2), (0, key1), (0, value1)])

            L_shared.done(pe, 0, 0)
            A_rows.done(pe, NB - 1)

            def shared_up(q, i):
                C_base.before(pe, q, i)
                S = C_gu.begin(pe, q, i)
                h = h2_all[:, span(batch(q, i), T)]
                for n, w in enumerate((Wg, Wu)):
                    for c in range(FC):
                        S(mm(bank[4 * q + n * FC + c][:], w[:, c * P:(c + 1) * P], h))

            def shared_down(q, i):
                C_act.done(pe, q, i)
                for c in range(FC):
                    last = mm(bank[4 * q][:], Wd[:, c], sg[q][c], start=c == 0, stop=c == FC - 1)
                C_dn.begin(pe, q, i)(last)

            def shared_pair(i):
                for q in range(2):
                    shared_up(q, i)
                for q in range(2):
                    shared_down(q, i)

            shared_up(0, 0)
            B_hot.done(pe, 0, 0)
            S = B_cnt.begin(pe, 0, 0)
            S(mm(bank[4][:], before_bf[:], onehot_b))
            S(mm(bank[5][:], ones_bf[:], onehot_b))
            B_slot.done(pe, 0, 0, 2)
            shared_up(1, 0)
            for q in range(2):
                shared_down(q, 0)
            with pe.Fori(1, PAIRS) as i:
                shared_pair(i)
            L_experts.done(pe, 0, 0)
            B_slot.done(pe, 0, 0)

            def row_in(j, q, i, old):
                D_x.done(pe, q, i)
                D_t.begin(pe, q, i)(pe.transpose(bank[q % 2][:, 0:P], xb[q][:, 0:P], ident[:]))

            def expert_of(j):
                e = pe.value_load(block_expert[0:1, bass.ds(j, 1)])
                return nc.s_assert_within(e, 0, E - 1, skip_runtime_bounds_check_because="phase B makes it as min(count, E-1)")

            ahead = {}

            def look_up(back):
                def stage(j, q, i, old):
                    ahead[back] = expert_of(j)
                return stage

            def gate_up(j, q, i, old):
                e = expert_of(j) if old else ahead[0]
                D_xT.done(pe, q, i)
                D_gu.begin(pe, q, i)(mm(bank[2 + q % 2][:], xbT[q % 2], up_experts[:, bass.ds(e, 1), :].rearrange("p o f -> p (o f)")))

            def turn_act(j, q, i, old):
                D_act.done(pe, q, i)
                for c in range(FC):
                    last = pe.transpose(bank[4 + q % 2][:, c * P:(c + 1) * P], acte[q % 2][:, c * P:(c + 1) * P], ident[:])
                D_at.begin(pe, q, i)(last)

            def down(j, q, i, old):
                e = ahead[3]
                D_aT.done(pe, q, i)
                if not isinstance(j, int) or j >= 2:
                    D_y.done(pe, (q - 2) % DEPTH, i + (q - 2) // DEPTH)
                for c in range(FC):
                    last = mm(bank[6 + q % 2][:, 0:C], aT[q % 2][:, c * P:(c + 1) * P],
                              down_experts[:, c, bass.ds(e, 1), :].rearrange("p o f -> p (o f)"), start=c == 0, stop=c == FC - 1)
                D_dn.begin(pe, q, i)(last)

            for q in range(2):
                C_base.done(pe, q, PAIRS - 1)
            blocks_of(pe, [(0, row_in), (1, gate_up), (0, look_up(0)), (3, look_up(3)), (2, turn_act), (3, down)])

            def y_turn(b, q, i):
                E_y.done(pe, q, i)
                E_f.before(pe, q, i)
                E_t.begin(pe, q, i)(turn(bank[q], flat(yt[q])))

            last_batches(pe, y_turn)


def kernel(**inputs):
    import concourse.bacc as bacc
    from concourse import mybir
    from concourse.bass_utils import run_bass_kernel_spmd

    def t(name):
        return np.ascontiguousarray(np.asarray(inputs[name]).T)

    x = np.ascontiguousarray(inputs["L0_attn_x"])
    nb, nt, c = x.shape
    vecs = ["L0_attn_ln1_g", "L0_attn_ln1_b", "L0_attn_ln2_g", "L0_attn_ln2_b", "L0_attn_att_time_mix",
            "L0_attn_att_combined_mix", "L0_attn_time_decay", "L0_attn_time_first", "L0_attn_ffn_time_mix",
            "L0_attn_ffn_combined_mix"]
    arrays = {
        "x": x,
        "xT": np.ascontiguousarray(x.reshape(nb * nt, c).T),
        "vecs": np.ascontiguousarray(np.stack([np.asarray(inputs[n]).reshape(c) for n in vecs], axis=1)),
        "cT": t("L0_c"),
        "wmod": np.ascontiguousarray(inputs["L0_wmod"]),
        "WkT": t("L0_attn_Wk"), "WvT": t("L0_attn_Wv"), "WrT": t("L0_attn_Wr"), "WoT": t("L0_attn_Wo"),
        "FkT": t("L0_attn_Fk"), "FvT": t("L0_attn_Fv"), "FrT": t("L0_attn_Fr"),
        "routerT": t("L0_ffn_w_router"),
        "gateT": t("L0_ffn_w_gate"), "upT": t("L0_ffn_w_up"), "downT": t("L0_ffn_w_down"),
        "gate_up": np.ascontiguousarray(inputs["L0_ffn_gate_up_proj"]),
        "down": np.ascontiguousarray(inputs["L0_ffn_down_proj"]),
    }
    nc = bacc.Bacc("TRN2", target_bir_lowering=False, num_devices=1)
    ins = {n: nc.dram_tensor(f"in_{n}", a.shape, mybir.dt.float32, kind="ExternalInput").ap() for n, a in arrays.items()}
    out_t = nc.dram_tensor("out_t", (c, nb * nt), mybir.dt.float32, kind="ExternalOutput").ap()
    program(nc, ins, out_t)
    got = run_bass_kernel_spmd(nc, [{f"in_{n}": a for n, a in arrays.items()}], core_ids=[0])
    return np.ascontiguousarray(got.results[0]["out_t"].T).reshape(nb, nt, c)
```

```python
import numpy as np


def program(nc, ins, out_t):
    import contextlib
    import concourse.bass as bass
    from concourse import mybir

    F32, I32, BF16 = mybir.dt.float32, mybir.dt.int32, mybir.dt.bfloat16
    ALU, ACT, AX = mybir.AluOpType, mybir.ActivationFunctionType, mybir.AxisListType

    NB, T, C = ins["x"].shape
    P = 128
    NT = T // P
    NTT = NB * NT
    PAIRS = NB // 2
    H = ins["FkT"].shape[1]
    HC = H // P
    CHUNKS = (0, 2, 1, 3)
    E = ins["routerT"].shape[1]
    F = ins["gateT"].shape[1]
    FC = F // P
    NBLK = NTT + E - 1
    ROW = C + 4
    NOROW = NB * T
    LAG = 3
    DEPTH = 6
    ENDS = 4
    DRAIN = 4
    EPS, KMAX = 1e-5, 60.0
    HALF = C // 2

    ctx = contextlib.ExitStack()
    with ctx:
        def sb(name, shape, dt=F32):
            return ctx.enter_context(nc.sbuf_tensor(name, shape, dt))

        ident = sb("ident", [P, P])
        ones_bf = sb("ones_bf", [P, P], BF16)
        before_bf = sb("before_bf", [P, P], BF16)
        vecs = sb("vecs", [P, 10])
        derived = sb("derived", [P, 12])
        modc = sb("modc", [P, 6, NB])
        small = sb("small", [P, 48])
        cT = sb("cT", [P, NB])
        sc = sb("sc", [P, NB])
        ca_rows = sb("ca_rows", [P, NB, C])
        sa_rows = sb("sa_rows", [P, NB, C])
        decay = sb("decay", [P, T])
        Wk = sb("Wk", [P, C]); Wv = sb("Wv", [P, C]); Wr = sb("Wr", [P, C]); Wo = sb("Wo", [P, C])
        Fk = sb("Fk", [P, H]); Fv = sb("Fv", [P, HC, C]); Fr = sb("Fr", [P, C])
        Wg = sb("Wg", [P, F]); Wu = sb("Wu", [P, F]); Wd = sb("Wd", [P, FC, C])
        router = sb("router", [P, E])
        h2_all = sb("h2_all", [P, NB * T])
        x3_all = sb("x3_all", [P, NB * T])
        rows = sb("rows", [P, NTT, ROW])
        logits = sb("logits", [P, NTT, E])
        top = sb("top", [P, NTT])
        slot_i = sb("slot_i", [P, NTT], I32)
        block_expert = sb("block_expert", [1, NBLK + 1], I32)
        up_experts = sb("up_experts", [P, E, 2 * F])
        down_experts = sb("down_experts", [P, FC, E, C])

        WORK = 27 * (T + 8)
        work = sb("work", [P, WORK])
        at = [0]

        def carve(n):
            a = at[0]
            at[0] += n
            assert at[0] <= WORK, (at[0], WORK)
            return work[:, a:a + n]

        def flat(t):
            return t.rearrange("p j c -> p (j c)")

        def two(n):
            return [carve(n), carve(n)]

        def tiles(ap):
            return ap.rearrange("p (j c) -> p j c", c=C)

        xtok, ht = tiles(carve(T)), tiles(carve(T))
        xT, xm, xm2 = carve(T), carve(T), carve(T)
        x1p, x2p = carve(T + 2), carve(T + 2)
        ek, er, kv, num, er2 = carve(T), carve(T), carve(T), carve(T), carve(T)
        apad, bpad = carve(T + 1), carve(T + 1)
        n3t, n4t = carve(T), carve(T)
        relus = [carve(T) for _ in range(HC)]
        h2w, x3w = carve(T), carve(T)
        stat = [carve(6 * NT) for _ in range(4)]
        mv = [carve(2 * NT).rearrange("p (j s) -> p j s", s=2) for _ in range(4)]
        rstd = [carve(NT) for _ in range(4)]
        shift = [carve(NT) for _ in range(4)]
        eexp = carve(NT)
        neghalf = sb("neghalf", [P, NT])
        one = sb("one", [P, 1])

        at[0] = 0
        G = NTT * E
        GX = E * (NTT + 1)
        rank = carve(G); cum = carve(GX); cand = carve(G)
        total = sb("total", [P, GX])[:]; seg = sb("seg", [P, GX])[:]
        onehot_b = carve(G // 2).bitcast(BF16)
        count_i = carve(E).bitcast(I32); bend = carve(E); nblk = carve(E); bstart = carve(E); best = carve(NTT); slot_f = carve(NTT)
        ltmp = carve(NBLK * E); esum = carve(NBLK)
        iota_e = sb("iota_e", [P, G])[:]
        iota_blk = sb("iota_blk", [P, NBLK * E])[:]; ones_e = sb("ones_e", [P, E])[:]
        sg = [[carve(T) for _ in range(FC)] for _ in range(2)]
        xb = [carve(ROW) for _ in range(DEPTH)]
        xbT = two(P)
        sge, acte, aT = two(F), two(F), two(F)
        yb = [carve(C) for _ in range(DEPTH)]
        number = [carve(1).bitcast(I32) for _ in range(DEPTH)]
        at[0] = 0
        yt = [tiles(carve(T)) for _ in range(ENDS)]; fin = [carve(T) for _ in range(ENDS)]
        pad_row = sb("pad_row", [P, ROW])

        bank = [ctx.enter_context(nc.psum_tensor(f"bank{n}", [P, 512], F32)) for n in range(8)]
        bR, bK, bV, bT2, bX2, bT3, bFK, bFK2 = range(8)
        bFV, bLG, bT1, bFR, bT4, bRT = bR, bK, bV, bT2, bX2, bT3
        shared_banks = ((bT1, bFR, bFK, bFK2), (bR, bK, bX2, bT3))
        tok = lambda n: bank[n][:].rearrange("p (j c) -> p j c", c=C)
        sorted_rows = nc.dram_tensor("sorted_rows", [NBLK * P, ROW], F32, kind="Internal").ap()
        y_rows = nc.dram_tensor("y_rows", [NB * T, C], F32, kind="Internal").ap()

        lone_waits = [ctx.enter_context(nc.semaphore(f"lone_waits{n}")) for n in range(2)]
        gpsimd = [None]

        def wait(eng, semaphore, value, alone=False):
            w = eng.wait_ge(semaphore, value)
            if not isinstance(value, int):
                if eng is gpsimd[0]:
                    w.then_inc(lone_waits[0], 1)
                elif alone:
                    w.then_inc(lone_waits[1], 1)

        class Steps:

            def __init__(self, name, n, slots=2, unit=1):
                self.n, self.unit = n * unit, unit
                self.sem = [ctx.enter_context(nc.semaphore(f"{name}{q}")) for q in range(slots)]
                self.count = 0

            def start(self, q, i):
                return i * self.n

            def at(self, q):
                return self.sem[q]

            def begin(self, eng, q, i):
                self.eng, self.q, self.i, self.count = eng, q, i, 0
                return self

            def __call__(self, instruction, then_wait=False):
                self.count += self.unit
                assert self.count <= self.n
                instruction.then_inc(self.at(self.q), self.unit)
                if then_wait:
                    wait(self.eng, self.at(self.q), self.start(self.q, self.i) + self.count, then_wait == "alone")

            def done(self, eng, q, i, part=None):
                wait(eng, self.at(q), self.start(q, i) + (self.n if part is None else part * self.unit))

            def before(self, eng, q, i):
                if not (isinstance(i, int) and i == 0):
                    wait(eng, self.at(q), self.start(0, i))

        class Turns(Steps):

            def __init__(self, name, n, places=2):
                super().__init__(name, n, 1)
                self.places = places

            def start(self, q, i):
                return (self.places * i + q) * self.n

            def at(self, q):
                return self.sem[0]

            def before(self, eng, q, i):
                if not (isinstance(i, int) and i == 0):
                    self.done(eng, q, i - 1)

        class Line(Steps):

            def __init__(self, name, n, unit=1):
                super().__init__(name, n, 1, unit)

            def begin(self, eng, b):
                return super().begin(eng, 0, b)

            def done(self, eng, b, part=None):
                super().done(eng, 0, b, part)

            def before(self, eng, b):
                super().before(eng, 0, b)

        def once(name, n, unit=1):
            return Steps(name, n, 1, unit)

        L_small = once("L_small", 2, 16)
        L_wmod = once("L_wmod", 1, 16)
        L_att = once("L_att", 5, 16)
        L_ffn = once("L_ffn", 3, 16)
        L_shared = once("L_shared", 4, 16)
        L_experts = once("L_experts", 3, 16)
        L_fill = once("L_fill", 1, 16)
        K_pool = once("K_pool", 16)
        K_dve = once("K_dve", 32)
        K_act = once("K_act", 5)
        K_pe = once("K_pe", 1 + NB // 2)
        K_rows = once("K_rows", NB // 2 * 2)
        A_x = Line("A_x", 1, unit=16)
        A_xT = Line("A_xT", 1, unit=16)
        A_st = [Line(f"A_st{n}_", 2 * NT) for n in range(4)]
        A_rs = [Line(f"A_rs{n}_", 4) for n in range(4)]
        A_n1 = Line("A_n1", NT)
        A_mod = Line("A_mod", 2)
        A_n2 = Line("A_n2", NT)
        A_t1 = Line("A_t1", 1)
        A_x1 = Line("A_x1", 2)
        A_mix = Line("A_mix", 2)
        A_kv = Line("A_kv", 2)
        A_r = Line("A_r", 1)
        A_tanh = Line("A_tanh", 1)
        A_exp = Line("A_exp", 1)
        A_wkv = Line("A_wkv", 8)
        A_cl = Line("A_cl", 1)
        A_wo = Line("A_wo", 1)
        A_n3 = Line("A_n3", NT)
        A_t2 = Line("A_t2", 1)
        A_x2 = Line("A_x2", 2)
        A_mix2 = Line("A_mix2", 2)
        A_fr = Line("A_fr", 1)
        A_fk = Line("A_fk", HC)
        A_relu = Line("A_relu", HC)
        A_sqa = Line("A_sqa", HC // 2)
        A_sqp = Line("A_sqp", HC // 2)
        A_fv = Line("A_fv", HC)
        A_th = Line("A_th", 1)
        A_x3 = Line("A_x3", 3)
        A_keep = Line("A_keep", 1)
        A_t3 = Line("A_t3", 1)
        A_n4 = Line("A_n4", NT)
        A_t4 = Line("A_t4", 1)
        A_h2 = Line("A_h2", 2)
        A_lg = Line("A_lg", 1)
        A_rt = Line("A_rt", 1)
        A_top = Line("A_top", 2)
        A_es = Line("A_es", 1)
        A_rows = Line("A_rows", 3)
        B_hot = once("B_hot", 4)
        B_cnt = once("B_cnt", 2)
        B_slot = once("B_slot", 18)
        B_pool = once("B_pool", 6)
        B_out = once("B_out", NTT, 16)
        C_gu = Turns("C_gu", 2 * FC)
        C_sg = Turns("C_sg", FC)
        C_act = Turns("C_act", FC)
        C_dn = Turns("C_dn", 1)
        C_base = Turns("C_base", 1)
        D_x = Steps("D_x", 1, DEPTH, 16)
        D_t = Turns("D_t", 1, DEPTH)
        D_xT = Turns("D_xT", 1, DEPTH)
        D_gu = Turns("D_gu", 1, DEPTH)
        D_sg = Turns("D_sg", 1, DEPTH)
        D_act = Turns("D_act", 2, DEPTH)
        D_at = Turns("D_at", 1, DEPTH)
        D_aT = Turns("D_aT", 1, DEPTH)
        D_dn = Turns("D_dn", 1, DEPTH)
        D_y = Turns("D_y", 1, DEPTH)
        D_out = Steps("D_out", 1, DEPTH, 16)
        E_y = Steps("E_y", 1, ENDS, unit=16)
        E_t = Turns("E_t", 1, ENDS)
        E_f = Turns("E_f", 1, ENDS)
        E_out = Steps("E_out", 1, ENDS, unit=16)

        g1, b1, g2, b2, tm1, cm1, tdec, tfirst, tm2, cm2 = (vecs[:, n:n + 1] for n in range(10))
        tg1, tb1, tg2, tb2, mA1, mA2, ed, eu, e_td, om1, om2, _ = (derived[:, n:n + 1] for n in range(12))
        SA, CA, GA, SB_, CB, GB = range(6)

        def batch(q, i):
            return 2 * i + q

        def slots(eng, stages):
            def slot(s):
                for group, stage in stages:
                    if not isinstance(s, int) or 0 <= s - group < NB:
                        stage(s - group)

            for s in range(LAG):
                slot(s)
            with eng.Fori(LAG, NB) as s:
                slot(s)
            for s in range(NB, NB + LAG):
                slot(s)

        def last_batches(eng, stage):
            for q in range(ENDS):
                stage(q, q, 0)
            with eng.Fori(1, NB // ENDS) as i:
                for q in range(ENDS):
                    stage(ENDS * i + q, q, i)

        def span(b, n):
            return bass.ds(b * n, n)

        def blocks_of(eng, stages, drain=DRAIN):
            def step(q, i):
                for back, stage in stages:
                    j = DEPTH * i + q - back
                    if not isinstance(i, int) or 0 <= j < NBLK:
                        stage(j, (q - back) % DEPTH, i + (q - back) // DEPTH)

            for q in range(DEPTH):
                step(q, 0)
            with eng.Fori(1, NBLK // DEPTH) as i:
                for q in range(DEPTH):
                    step(q, i)
            for q in range(NBLK % DEPTH + drain):
                step(q, NBLK // DEPTH)

        block = ctx.enter_context(nc.Block())

        @block.sync
        def _(sp):
            def tokens(t, b):
                return t[b].rearrange("(j p) c -> p j c", p=P)

            def load(step, dst, src):
                step(sp.dma_start(dst, src))

            for s in (L_small, L_wmod, L_att, L_ffn, L_shared, L_experts, L_fill):
                s.begin(sp, 0, 0)
            load(L_small, cT[:], ins["cT"])
            load(L_small, vecs[:], ins["vecs"])
            load(L_wmod, up_experts[:, 0:2, :].rearrange("p a b -> p (a b)")[:, 0:6 * C], ins["wmod"])
            A_x.begin(sp, 0)(sp.dma_start(xtok, tokens(ins["x"], 0)))
            for w, n in ((Wk, "WkT"), (Wv, "WvT"), (Wr, "WrT"), (Wo, "WoT")):
                load(L_att, w[:], ins[n])
            load(L_att, router[:], ins["routerT"])
            load(L_ffn, Fk[:], ins["FkT"])
            load(L_ffn, Fv[:], ins["FvT"].rearrange("(k p) c -> p k c", p=P))
            load(L_ffn, Fr[:], ins["FrT"])
            A_xT.begin(sp, 0)(sp.dma_start(xT, ins["xT"][:, 0:T]))

            def refill_x(b):
                A_n1.before(sp, b)
                A_x.begin(sp, b)(sp.dma_start(xtok, tokens(ins["x"], b)))

            def refill_xT(b):
                A_x3.before(sp, b)
                A_xT.begin(sp, b)(sp.dma_start(xT, ins["xT"][:, span(b, T)]))

            refill_x(1)
            load(L_shared, Wg[:], ins["gateT"])
            load(L_shared, Wu[:], ins["upT"])
            load(L_shared, Wd[:], ins["downT"].rearrange("(k p) c -> p k c", p=P))
            load(L_shared, down_experts[:, 0], ins["down"][:, 0:P, :].rearrange("e p c -> p e c"))
            load(L_experts, down_experts[:, 1], ins["down"][:, P:2 * P, :].rearrange("e p c -> p e c"))
            refill_x(2)
            K_rows.done(sp, 0, 0)
            load(L_experts, up_experts[:, 0:E // 2, :], ins["gate_up"][0:E // 2].rearrange("e p f -> p e f"))
            load(L_experts, up_experts[:, E // 2:, :], ins["gate_up"][E // 2:].rearrange("e p f -> p e f"))
            with sp.Fori(LAG, NB) as s:
                refill_x(s)
                refill_xT(s - LAG + 1)
            K_pool.done(sp, 0, 0)
            load(L_fill, sorted_rows.rearrange("(k p) r -> p k r", p=P),
                 pad_row[:].rearrange("p (o r) -> p o r", o=1).broadcast_to([P, NBLK, ROW]))
            for b in range(NB - LAG + 1, NB):
                refill_xT(b)

            B_out.done(sp, 0, 0)

            def block_in(j, q, i):
                if not (isinstance(i, int) and i == 0):
                    D_act.done(sp, q, i - 1)
                D_x.begin(sp, q, i)(sp.dma_start(xb[q], sorted_rows[span(j, P), :]))

            blocks_of(sp, [(0, block_in)], 0)

            for q in range(DEPTH):
                D_out.done(sp, q, (NBLK - 1 - q) // DEPTH)
            def y_in(b, q, i):
                E_t.before(sp, q, i)
                E_y.begin(sp, q, i)(sp.dma_start(yt[q], y_rows[span(b, T), :].rearrange("(j p) c -> p j c", p=P)))

            last_batches(sp, y_in)

        @block.gpsimd
        def _(pool):
            K = K_pool.begin(pool, 0, 0)
            gpsimd[0] = pool
            K(pool.memset(one[:], 1.0))
            K(pool.memset(ident[:], 0.0))
            K(pool.memset(neghalf[:], -0.5), True)
            K(pool.affine_select(out=ident[:], in_=ident[:], compare_op=ALU.not_equal, fill=1.0, base=0,
                                 pattern=[[-1, P]], channel_multiplier=1))
            K(pool.memset(ones_bf[:], 1.0), True)
            K(pool.affine_select(out=before_bf[:], in_=ones_bf[:], compare_op=ALU.is_gt, fill=0.0, base=0,
                                 pattern=[[1, P]], channel_multiplier=-1))
            K(pool.memset(pad_row[:, 0:C], 0.0))
            K(pool.memset(pad_row[:, C:ROW].bitcast(I32), NOROW))
            K(pool.iota(rows[:, :, C:C + 1].bitcast(I32), pattern=[[P, NTT], [1, 1]], base=0, channel_multiplier=1))
            K(pool.memset(rows[:, :, C + 1:ROW], 0.0))
            for t in (x1p, x2p):
                K(pool.memset(t[:, 0:1], 0.0))
                K(pool.memset(t[:, T + 1:T + 2], 0.0))
            for t in (apad, bpad):
                K(pool.memset(t[:, 0:1], 0.0))
            assert K.count == K.n
            S = B_pool.begin(pool, 0, 0)
            small_ints = dict(allow_small_or_imprecise_dtypes=True)
            S(pool.iota(iota_e, pattern=[[0, NTT], [-1, E]], base=E, channel_multiplier=0, **small_ints))
            S(pool.iota(iota_blk, pattern=[[1, NBLK], [0, E]], base=0, channel_multiplier=0, **small_ints))
            S(pool.memset(ones_e, 1.0))
            S(pool.memset(seg, 1.0), True)
            S(pool.memset(seg.rearrange("p (e n) -> p e n", e=E)[:, :, 0:1], 0.0))
            S(pool.memset(total.rearrange("p (e n) -> p e n", e=E)[:, :, 0:1], 0.0))

            def rs(n):
                def stage(b):
                    A_st[n].done(pool, b)
                    S = A_rs[n].begin(pool, b)
                    S(pool.tensor_scalar(rstd[n], mv[n][:, :, 1], EPS, None, ALU.add), True)
                    S(pool.tensor_tensor(rstd[n], rstd[n], neghalf[:], ALU.pow), True)
                    S(pool.tensor_scalar(shift[n], mv[n][:, :, 0], -1.0, None, ALU.mult), True)
                    S(pool.tensor_tensor(shift[n], shift[n], rstd[n], ALU.mult))
                return stage

            def modulate(b):
                if isinstance(b, int) and b % 2 == 0:
                    K_rows.done(pool, 0, 0, None if b else 2)
                A_n1.done(pool, b)
                S = A_mod.begin(pool, b)
                row = lambda t: t[:, bass.ds(b, 1), :].broadcast_to([P, NT, C])
                S(pool.tensor_tensor(ht, ht, row(ca_rows), ALU.mult), True)
                S(pool.tensor_tensor(ht, ht, row(sa_rows), ALU.add))

            def square(c):
                def stage(b):
                    if c == 1:
                        A_sqp.begin(pool, b)
                    A_relu.done(pool, b, CHUNKS.index(c) + 1)
                    A_sqp(pool.tensor_tensor(relus[c], relus[c], relus[c], ALU.mult))
                return stage

            slots(pool, [(1, rs(1)), (3, square(1)), (3, square(3)), (0, rs(0)), (2, rs(2)), (0, modulate), (3, rs(3))])

            A_rows.done(pool, NB - 1)
            L_fill.done(pool, 0, 0)
            B_slot.done(pool, 0, 0, 13)
            S = B_out.begin(pool, 0, 0)
            for n in range(NTT):
                S(pool.indirect_dma_start(sorted_rows, bass.IndirectOffsetOnAxis(slot_i[:, n:n + 1], 0), rows[:, n, :], None))

            def block_out(j, q, i):
                D_y.done(pool, q, i)
                D_out.begin(pool, q, i)(pool.indirect_dma_start(
                    y_rows, bass.IndirectOffsetOnAxis(number[q], 0), yb[q], None,
                    bounds_check=NB * T - 1, oob_is_err=False))

            blocks_of(pool, [(0, block_out)], 0)

        @block.vector
        def _(dve):
            def stats(n, b, src):
                S = A_st[n].begin(dve, b)
                s6 = stat[n].rearrange("p (j s) -> p j s", s=6)
                for j in range(NT):
                    S(dve.bn_stats(s6[:, j], src[:, j]), j == NT - 1 and "alone")
                for j in range(NT):
                    S(dve.bn_aggr(mv[n][:, j], s6[:, j]))

            K = K_dve.begin(dve, 0, 0)
            L_small.done(dve, 0, 0)
            K_act.done(dve, 0, 0, 1)
            K(dve.tensor_scalar(sc[:], sc[:], 1.0, None, ALU.add), True)
            K(dve.reciprocal(sc[:], sc[:]), True)
            K(dve.tensor_tensor(sc[:], sc[:], cT[:], ALU.mult), True)
            scb = h2_all[:].rearrange("p (b c) -> p b c", c=T)[:, :, 0:P]
            K(dve.tensor_copy(scb, sc[:].rearrange("p (b o) -> p b o", o=1).broadcast_to([P, NB, P])))
            K_act.done(dve, 0, 0, 4)
            K(dve.tensor_scalar(om1, tm1, -1.0, 1.0, ALU.mult, ALU.add), True)
            K(dve.tensor_scalar(om2, tm2, -1.0, 1.0, ALU.mult, ALU.add), True)
            K(dve.tensor_copy(mA1, om1))
            K(dve.tensor_copy(mA2, om2), True)
            K(dve.tensor_tensor(mA1[0:HALF], om1[0:HALF], cm1[0:HALF], ALU.add))
            K(dve.tensor_tensor(mA2[0:HALF], om2[0:HALF], cm2[0:HALF], ALU.add))
            K(dve.tensor_tensor(tg1, tm1, g1, ALU.mult))
            K(dve.tensor_tensor(tb1, tm1, b1, ALU.mult))
            K(dve.tensor_tensor(tg2, tm2, g2, ALU.mult))
            K(dve.tensor_tensor(tb2, tm2, b2, ALU.mult))
            K(dve.memset(decay[:], 1.0), True)
            K(dve.tensor_scalar(decay[:], decay[:], ed, None, ALU.mult))
            A_x.done(dve, 0)
            stats(0, 0, xtok)
            K_pe.done(dve, 0, 0, 1)
            K(dve.tensor_copy(modc[:], bank[0][:, 0:6 * NB].rearrange("p (n b) -> p n b", b=NB)), True)
            for n in (CA, CB):
                K(dve.tensor_scalar(modc[:, n], modc[:, n], 1.0, None, ALU.add))
            for n, s in ((GA, small[:, 0:2 * NB]), (GB, small[:, 2 * NB:4 * NB])):
                sign, mag = s[:, 0:NB], s[:, NB:2 * NB]
                K(dve.tensor_scalar(sign, modc[:, n], 0.0, 2.0, ALU.is_ge, ALU.mult), True)
                K(dve.tensor_scalar(sign, sign, -1.0, None, ALU.add), True)
                K(dve.tensor_scalar(mag, modc[:, n], -1.0, None, ALU.mult), True)
                K(dve.tensor_tensor(mag, mag, modc[:, n], ALU.max), True)
                K(dve.tensor_scalar(mag, mag, 0.25, None, ALU.max), True)
                K(dve.tensor_tensor(modc[:, n], mag, sign, ALU.mult), True)
            L_att.done(dve, 0, 0)
            K(dve.tensor_scalar(Wo[:], Wo[:], 0.5, None, ALU.mult), True)
            assert K.count == K.n
            K_pool.done(dve, 0, 0)

            def norm1_stats(b):
                if isinstance(b, int) and b == 0:
                    return
                A_x.done(dve, b)
                stats(0, b, xtok)

            def norm2_stats(b):
                A_mod.done(dve, b)
                stats(1, b, ht)

            def mix(step, xmix, xp, mA, cm, b):
                S = step.begin(dve, b)
                S(dve.scalar_tensor_tensor(xmix, xp[:, 0:T], mA, xmix, ALU.mult, ALU.add), True)
                S(dve.scalar_tensor_tensor(xmix[HALF:], xp[HALF:, 2:T + 2], cm[HALF:], xmix[HALF:], ALU.mult, ALU.add))

            def mix1(b):
                A_x1.done(dve, b)
                mix(A_mix, xm, x1p, mA1, cm1, b)

            def mix2(b):
                A_x2.done(dve, b)
                mix(A_mix2, xm2, x2p, mA2, cm2, b)

            def clamp(b):
                A_kv.done(dve, b, 1)
                A_cl.begin(dve, b)(dve.tensor_scalar(ek, bank[bK][:], KMAX, None, ALU.min))

            def wkv_scans(b):
                A_exp.done(dve, b)
                A_kv.done(dve, b)
                S = A_wkv.begin(dve, b)
                S(dve.tensor_tensor(kv, ek, bank[bV][:], ALU.mult))
                S(dve.tensor_tensor_scan(bpad[:, 1:T + 1], decay[:], ek, 0.0, ALU.mult, ALU.add), True)
                S(dve.tensor_tensor_scan(apad[:, 1:T + 1], decay[:], kv, 0.0, ALU.mult, ALU.add))
                S(dve.scalar_tensor_tensor(ek, ek, eu, bpad[:, 0:T], ALU.mult, ALU.add), True)
                S(dve.scalar_tensor_tensor(num, kv, eu, apad[:, 0:T], ALU.mult, ALU.add))

            def wkv_divide(b):
                A_tanh.done(dve, b)
                S = A_wkv
                S(dve.reciprocal(ek, ek), True)
                S(dve.scalar_tensor_tensor(num, er, 1.0, num, ALU.add, ALU.mult), True)
                S(dve.tensor_tensor(num, num, ek, ALU.mult))

            def norm3_stats(b):
                A_wo.done(dve, b)
                stats(2, b, tok(bX2))

            def residual(b):
                A_th.done(dve, b)
                A_fv.done(dve, b)
                A_xT.done(dve, b)
                S = A_x3.begin(dve, b)
                S(dve.scalar_tensor_tensor(er2, er2, 1.0, bank[bFV][:], ALU.add, ALU.mult), True)
                S(dve.scalar_tensor_tensor(er2, er2, 0.5, x2p[:, 1:T + 1], ALU.mult, ALU.add), True)
                S(dve.scalar_tensor_tensor(x3w, er2, modc[:, GA, bass.ds(b, 1)], xT, ALU.mult, ALU.add))

            def norm4_stats(b):
                A_t3.done(dve, b)
                stats(3, b, tok(bT3))

            def top_logit(b):
                A_lg.done(dve, b)
                S = A_top.begin(dve, b)
                lg = bank[bLG][:, 0:NT * E].rearrange("p (j e) -> p j e", e=E)
                S(dve.tensor_copy(logits[:, span(b, NT), :], lg))
                S(dve.tensor_reduce(top[:, span(b, NT)], lg, AX.X, ALU.max))

            def scored_rows(b):
                A_es.done(dve, b)
                S = A_rows.begin(dve, b)
                S(dve.tensor_scalar(eexp, eexp, 1.0, None, ALU.add), True)
                S(dve.reciprocal(eexp, eexp), True)
                A_rt.done(dve, b)
                S(dve.tensor_tensor(rows[:, span(b, NT), 0:C], tok(bRT),
                                    eexp.rearrange("p (j o) -> p j o", o=1).broadcast_to([P, NT, C]), ALU.mult))

            slots(dve, [(0, norm1_stats), (2, norm3_stats), (1, mix1), (3, residual), (1, clamp), (3, norm4_stats),
                        (0, norm2_stats), (2, mix2), (1, wkv_scans), (1, wkv_divide), (3, top_logit), (3, scored_rows)])

            B_pool.done(dve, 0, 0)
            A_top.done(dve, NB - 1)
            te = lambda t: t.rearrange("p (n e) -> p n e", e=E)
            et = lambda t: te(t).rearrange("p n e -> p e n")
            over = lambda t, n: t.rearrange("p (n o) -> p n o", o=1).broadcast_to([P, NTT, n])
            S = B_hot.begin(dve, 0, 0)
            S(dve.tensor_tensor(te(cand), logits[:], over(top[:], E), ALU.is_equal), True)
            S(dve.tensor_tensor(cand, cand, iota_e, ALU.mult), True)
            S(dve.tensor_reduce(best, te(cand), AX.X, ALU.max), True)
            S(dve.tensor_tensor(te(onehot_b), te(iota_e), over(best, E), ALU.is_equal), True)

            def shared_act(q, i):
                S = C_act.begin(dve, q, i)
                for c in range(FC):
                    C_sg.done(dve, q, i, c + 1)
                    C_gu.done(dve, q, i, FC + c + 1)
                    S(dve.tensor_tensor(sg[q][c], sg[q][c], bank[shared_banks[q][FC + c]][:], ALU.mult))

            def shared_base(q, i):
                b = batch(q, i)
                C_dn.done(dve, q, i)
                x3 = x3_all[:, span(b, T)]
                C_base.begin(dve, q, i)(dve.scalar_tensor_tensor(
                    x3, bank[shared_banks[q][0]][:], modc[:, GB, bass.ds(b, 1)], x3, ALU.mult, ALU.add))

            def shared_pair(i):
                for q in range(2):
                    shared_act(q, i)
                for q in range(2):
                    shared_base(q, i)

            shared_act(0, 0)
            S = B_slot.begin(dve, 0, 0)
            B_cnt.done(dve, 0, 0)
            S(dve.tensor_copy(total.rearrange("p (e n) -> p e n", e=E)[:, :, 1:], et(bank[bT3][:])), True)
            S(dve.tensor_tensor_scan(cum, seg, total, 0.0, ALU.mult, ALU.add), True)
            cum3 = cum.rearrange("p (e n) -> p e n", e=E)
            S(dve.tensor_scalar(count_i.rearrange("p (e o) -> p e o", o=1), cum3[:, :, NTT:], float(P - 1), None, ALU.add), True)
            S(dve.tensor_scalar(count_i, count_i, P.bit_length() - 1, None, ALU.logical_shift_right), True)
            S(dve.tensor_copy(nblk, count_i), True)
            S(dve.tensor_tensor_scan(bend, ones_e, nblk, 0.0, ALU.mult, ALU.add), True)
            S(dve.tensor_tensor(bstart, bend, nblk, ALU.subtract), True)
            S(dve.tensor_scalar(bstart, bstart, float(P), None, ALU.mult), True)
            S(dve.tensor_tensor(te(rank), te(bank[bX2][:]), cum3[:, :, 0:NTT].rearrange("p e n -> p n e"), ALU.add), True)
            S(dve.tensor_tensor(te(rank), te(rank), bstart.rearrange("p (o e) -> p o e", o=1).broadcast_to([P, NTT, E]), ALU.add), True)
            S(dve.tensor_tensor(rank, rank, onehot_b, ALU.mult), True)
            S(dve.tensor_reduce(slot_f, te(rank), AX.X, ALU.add), True)
            S(dve.tensor_copy(slot_i[:], slot_f), True)
            shared_base(0, 0)
            shared_act(1, 0)
            shared_base(1, 0)
            S(dve.tensor_tensor(ltmp[0:1].rearrange("p (j e) -> p j e", e=E),
                                bend[0:1].rearrange("p (o e) -> p o e", o=1).broadcast_to([1, NBLK, E]),
                                iota_blk[0:1].rearrange("p (j e) -> p j e", e=E), ALU.is_le), True)
            S(dve.tensor_reduce(esum[0:1], ltmp[0:1].rearrange("p (j e) -> p j e", e=E), AX.X, ALU.add), True)
            S(dve.tensor_scalar(esum[0:1], esum[0:1], float(E - 1), None, ALU.min), True)
            S(dve.memset(block_expert[:, NBLK:], 0))
            S(dve.tensor_copy(block_expert[:, 0:NBLK], esum[0:1]), True)
            assert S.count == S.n

            with dve.Fori(1, PAIRS) as i:
                shared_pair(i)

            def expert_act(j, q, i):
                D_out.before(dve, q, i)
                S = D_act.begin(dve, q, i)
                D_sg.done(dve, q, i)
                S(dve.tensor_copy(number[q], xb[q][:, C:C + 1].bitcast(I32)))
                S(dve.tensor_tensor(acte[q % 2], sge[q % 2], bank[2 + q % 2][:, F:2 * F], ALU.mult))

            def expert_aT(j, q, i):
                D_at.done(dve, q, i)
                D_aT.begin(dve, q, i)(dve.tensor_copy(aT[q % 2], bank[4 + q % 2][:, 0:F]))

            blocks_of(dve, [(2, expert_aT), (1, expert_act)])

            def last_residual(b, q, i):
                E_t.done(dve, q, i)
                E_out.before(dve, q, i)
                E_f.begin(dve, q, i)(dve.scalar_tensor_tensor(
                    fin[q], bank[q][:], modc[:, GB, bass.ds(b, 1)], x3_all[:, span(b, T)], ALU.mult, ALU.add))

            last_batches(dve, last_residual)

        @block.scalar
        def _(act):
            K = K_act.begin(act, 0, 0)
            L_small.done(act, 0, 0)
            K(act.activation(sc[:], cT[:], ACT.Exp, scale=-1.0))
            K(act.activation(e_td, tdec, ACT.Exp), True)
            K(act.activation(eu, tfirst, ACT.Exp))
            K(act.activation(ed, e_td, ACT.Exp, scale=-1.0))
            K(act.activation(small[:, 40:41], tfirst, ACT.Tanh))
            R = K_rows.begin(act, 0, 0)
            K_pool.done(act, 0, 0)

            def modulation_rows(n):
                K_pe.done(act, 0, 0, 2 + n)
                v = bank[1 + n][:].rearrange("p (b m c) -> p b m c", b=2, m=2)
                R(act.copy(sa_rows[:, 2 * n:2 * n + 2, :], v[:, :, 0]))
                R(act.activation(ca_rows[:, 2 * n:2 * n + 2, :], v[:, :, 1], ACT.Identity, bias=one[:]))

            def other_rows(b):
                if isinstance(b, int) and b == 0:
                    for n in range(1, NB // 2):
                        modulation_rows(n)
                    K_dve.done(act, 0, 0)

            modulation_rows(0)

            def affine(dst, src, scale, bias):
                return act.activation(dst, src, ACT.Identity, bias=bias, scale=scale)

            def x1(b):
                A_t1.done(act, b)
                A_wo.before(act, b)
                S = A_x1.begin(act, b)
                S(affine(x1p[:, 1:T + 1], bank[bT1][:], g1, b1))
                S(affine(xm, bank[bT1][:], tg1, tb1))

            def tanh_r(b):
                A_r.done(act, b)
                A_wkv.before(act, b)
                A_tanh.begin(act, b)(act.activation(er, bank[bR][:], ACT.Tanh, scale=0.5))

            def exp_k(b):
                A_cl.done(act, b)
                A_exp.begin(act, b)(act.activation(ek, ek, ACT.Exp))

            def norm_rows(step, n, b, src, dst):
                A_rs[n].done(act, b)
                S = step.begin(act, b)
                for j in range(NT):
                    S(affine(dst[:, j * C:(j + 1) * C], src[:, j * C:(j + 1) * C], rstd[n][:, j:j + 1],
                             shift[n][:, j:j + 1]))

            def norm1(b):
                norm_rows(A_n1, 0, b, flat(xtok), flat(ht))

            def norm2(b):
                norm_rows(A_n2, 1, b, flat(ht), flat(ht))

            def norm3(b):
                norm_rows(A_n3, 2, b, bank[bX2], n3t)

            def norm4(b):
                norm_rows(A_n4, 3, b, bank[bT3], n4t)

            def x2(b):
                A_t2.done(act, b)
                S = A_x2.begin(act, b)
                S(affine(x2p[:, 1:T + 1], bank[bT2][:], g2, b2))
                S(affine(xm2, bank[bT2][:], tg2, tb2))

            def tanh_r2(b):
                A_fr.done(act, b)
                A_th.begin(act, b)(act.activation(er2, bank[bFR][:], ACT.Tanh, scale=0.5))

            def relu(c):
                k = CHUNKS.index(c)

                def stage(b):
                    if k == 0:
                        A_relu.begin(act, b)
                    A_fk.done(act, b, k + 1)
                    A_relu(act.activation(relus[c], bank[(bFK, bFK2)[k % 2]][:], ACT.Relu))
                return stage

            def square(c):
                def stage(b):
                    if c == 0:
                        A_sqa.begin(act, b)
                    A_relu.done(act, b, CHUNKS.index(c) + 1)
                    A_sqa(act.activation(relus[c], relus[c], ACT.Square))
                return stage

            def keep_x3(b):
                A_x3.done(act, b)
                A_keep.begin(act, b)(act.copy(x3_all[:, span(b, T)], x3w))

            def h2(b):
                A_t4.done(act, b)
                S = A_h2.begin(act, b)
                s, t = modc[:, CB, bass.ds(b, 1)], modc[:, SB_, bass.ds(b, 1)]
                S(affine(h2w, bank[bT4][:], s, t))
                S(affine(h2_all[:, span(b, T)], bank[bT4][:], s, t))

            def exp_top(b):
                A_top.done(act, b)
                A_es.begin(act, b)(act.activation(eexp, top[:, span(b, NT)], ACT.Exp, scale=-1.0))

            slots(act, [(0, norm1), (0, other_rows), (2, norm3), (2, x2), (1, exp_k), (3, keep_x3), (3, norm4), (1, tanh_r), (2, relu(0)),
                        (3, h2), (2, relu(2)), (0, norm2), (2, square(0)), (2, relu(1)), (2, relu(3)), (2, square(2)),
                        (3, exp_top), (0, x1), (2, tanh_r2)])

            def shared_silu(i):
                if isinstance(i, int):
                    A_rows.done(act, NB - 1)
                for q in range(2):
                    S = C_sg.begin(act, q, i)
                    C_dn.before(act, q, i)
                    for c in range(FC):
                        C_gu.done(act, q, i, c + 1)
                        S(act.activation(sg[q][c], bank[shared_banks[q][c]][:], ACT.Silu))

            shared_silu(0)
            with act.Fori(1, PAIRS) as i:
                shared_silu(i)

            def expert_xT(j, q, i):
                D_t.done(act, q, i)
                D_xT.begin(act, q, i)(act.copy(xbT[q % 2], bank[q % 2][:, 0:P]))

            def expert_silu(j, q, i):
                D_gu.done(act, q, i)
                D_sg.begin(act, q, i)(act.activation(sge[q % 2], bank[2 + q % 2][:, 0:F], ACT.Silu))

            def expert_y(j, q, i):
                D_dn.done(act, q, i)
                D_out.before(act, q, i)
                D_y.begin(act, q, i)(act.copy(yb[q], bank[6 + q % 2][:, 0:C]))

            blocks_of(act, [(0, expert_xT), (1, expert_silu), (3, expert_y)])

            def store(b, q, i):
                E_f.done(act, q, i)
                E_out.begin(act, q, i)(act.dma_start(out_t[:, span(b, T)], fin[q]))

            last_batches(act, store)
            for q in range(ENDS):
                E_out.done(act, q, NB // ENDS - 1)

        @block.tensor
        def _(pe):
            K_dve.done(pe, 0, 0, 4)
            L_wmod.done(pe, 0, 0)
            K = K_pe.begin(pe, 0, 0)
            wmod = up_experts[:, 0:2, :].rearrange("p a b -> p (a b)")[:, 0:6 * C]
            scb = h2_all[:].rearrange("p (b c) -> p b c", c=T)[:, :, 0:P]
            for n in range(6):
                last = pe.matmul(bank[0][:, n * NB:(n + 1) * NB], wmod[:, n * C:(n + 1) * C], sc[:], start=True, stop=True)
            K(last)
            for b in range(NB):
                last = pe.matmul(bank[1 + b // 2][:, b % 2 * 2 * C:(b % 2 + 1) * 2 * C], scb[:, b], wmod[:, 0:2 * C], start=True, stop=True)
                if b % 2:
                    K(last)
            K_pool.done(pe, 0, 0)
            K_rows.done(pe, 0, 0)
            K_dve.done(pe, 0, 0)
            for s in (L_att, L_ffn, L_small):
                s.done(pe, 0, 0)

            def turn(out, src, **kw):
                for j in range(NT):
                    last = pe.transpose(out[:, j * P:(j + 1) * P], src[:, j * P:(j + 1) * P], ident[:])
                return last

            def mm(out, w, x, start=True, stop=True):
                return pe.matmul(out, w, x, start=start, stop=stop)

            def t1(b):
                A_n2.done(pe, b)
                if not (isinstance(b, int) and b == 0):
                    A_wkv.done(pe, b - 1, 1)
                A_t1.begin(pe, b)(turn(bank[bT1], flat(ht)))

            def key1(b):
                A_mix.done(pe, b)
                A_kv.begin(pe, b)(mm(bank[bK][:], Wk[:], xm))

            def value1(b):
                A_kv(mm(bank[bV][:], Wv[:], xm))

            def gate1(b):
                A_r.begin(pe, b)(mm(bank[bR][:], Wr[:], xm))

            def wo(b):
                A_wkv.done(pe, b)
                for j in range(NT):
                    o, c = bank[bX2][:, j * P:(j + 1) * P], slice(j * P, (j + 1) * P)
                    pe.matmul(o, x1p[:, 1 + j * P:1 + (j + 1) * P], ident[:], start=True, stop=False, is_transpose=True)
                    last = mm(o, num[:, c], Wo[:], start=False)
                A_wo.begin(pe, b)(last)

            def t2(b):
                A_n3.done(pe, b)
                A_t2.begin(pe, b)(turn(bank[bT2], n3t))

            def key2(k):
                c = CHUNKS[k]

                def stage(b):
                    if k == 0:
                        A_mix2.done(pe, b)
                        A_fk.begin(pe, b)
                    elif k >= 2:
                        A_relu.done(pe, b, k - 1)
                    A_fk(mm(bank[(bFK, bFK2)[k % 2]][:], Fk[:, c * P:(c + 1) * P], xm2))
                return stage

            def gate2(b):
                A_fr.begin(pe, b)(mm(bank[bFR][:], Fr[:], xm2))

            def values2(*chunks):
                def stage(b):
                    if chunks[0] == 0:
                        A_fv.begin(pe, b)
                    for c in chunks:
                        (A_sqa if c % 2 == 0 else A_sqp).done(pe, b, c // 2 + 1)
                        A_fv(mm(bank[bFV][:], Fv[:, c], relus[c], start=c == 0, stop=c == HC - 1))
                return stage

            def t3(b):
                A_x3.done(pe, b)
                A_t3.begin(pe, b)(turn(bank[bT3], x3w))

            def t4(b):
                A_n4.done(pe, b)
                A_t4.begin(pe, b)(turn(bank[bT4], n4t))

            def route(b):
                A_h2.done(pe, b)
                for j in range(NT):
                    last = mm(bank[bLG][:, j * E:(j + 1) * E], h2w[:, j * P:(j + 1) * P], router[:])
                A_lg.begin(pe, b)(last)

            def back(b):
                A_rt.begin(pe, b)(turn(bank[bRT], h2w))

            def shared_up(q, i):
                C_base.before(pe, q, i)
                S = C_gu.begin(pe, q, i)
                h = h2_all[:, span(batch(q, i), T)]
                for n, w in enumerate((Wg, Wu)):
                    for c in range(FC):
                        S(mm(bank[shared_banks[q][n * FC + c]][:], w[:, c * P:(c + 1) * P], h))

            def first_shared(b):
                if isinstance(b, int) and b == NB - 1:
                    L_shared.done(pe, 0, 0)
                    shared_up(0, 0)

            slots(pe, [(2, key2(0)), (3, first_shared), (3, t4), (2, key2(1)), (2, key2(2)), (2, gate2), (3, route), (2, key2(3)), (0, t1),
                       (3, back), (2, values2(0)), (1, wo), (2, values2(1, 2, 3)), (0, key1), (2, t3), (1, t2),
                       (0, value1), (0, gate1)])

            A_rows.done(pe, NB - 1)

            def shared_down(q, i):
                C_act.done(pe, q, i)
                for c in range(FC):
                    last = mm(bank[shared_banks[q][0]][:], Wd[:, c], sg[q][c], start=c == 0, stop=c == FC - 1)
                C_dn.begin(pe, q, i)(last)

            def shared_pair(i):
                for q in range(2):
                    shared_up(q, i)
                for q in range(2):
                    shared_down(q, i)

            B_hot.done(pe, 0, 0)
            S = B_cnt.begin(pe, 0, 0)
            S(mm(bank[bX2][:], before_bf[:], onehot_b))
            S(mm(bank[bT3][:], ones_bf[:], onehot_b))
            shared_down(0, 0)
            B_slot.done(pe, 0, 0, 9)
            shared_up(1, 0)
            shared_down(1, 0)
            with pe.Fori(1, PAIRS) as i:
                shared_pair(i)
            L_experts.done(pe, 0, 0)
            B_slot.done(pe, 0, 0)

            def row_in(j, q, i):
                D_x.done(pe, q, i)
                D_t.begin(pe, q, i)(pe.transpose(bank[q % 2][:, 0:P], xb[q][:, 0:P], ident[:]))

            def expert_of(j):
                e = pe.value_load(block_expert[0:1, bass.ds(j, 1)])
                return nc.s_assert_within(e, 0, E - 1, skip_runtime_bounds_check_because="phase B makes it as min(count, E-1)")

            experts = {}

            def look_up(back):
                def stage(j, q, i):
                    experts[back] = expert_of(j)
                return stage

            def gate_up(j, q, i):
                e = experts[1]
                D_xT.done(pe, q, i)
                D_gu.begin(pe, q, i)(mm(bank[2 + q % 2][:], xbT[q % 2], up_experts[:, bass.ds(e, 1), :].rearrange("p o f -> p (o f)")))

            def turn_act(j, q, i):
                D_act.done(pe, q, i)
                for c in range(FC):
                    last = pe.transpose(bank[4 + q % 2][:, c * P:(c + 1) * P], acte[q % 2][:, c * P:(c + 1) * P], ident[:])
                D_at.begin(pe, q, i)(last)

            def down(j, q, i):
                e = experts[4]
                D_aT.done(pe, q, i)
                if not isinstance(j, int) or j >= 2:
                    D_y.done(pe, (q - 2) % DEPTH, i + (q - 2) // DEPTH)
                for c in range(FC):
                    last = mm(bank[6 + q % 2][:, 0:C], aT[q % 2][:, c * P:(c + 1) * P],
                              down_experts[:, c, bass.ds(e, 1), :].rearrange("p o f -> p (o f)"), start=c == 0, stop=c == FC - 1)
                D_dn.begin(pe, q, i)(last)

            for q in range(2):
                C_base.done(pe, q, PAIRS - 1)
            blocks_of(pe, [(1, look_up(1)), (4, look_up(4)), (3, turn_act), (4, down), (0, row_in), (1, gate_up)])

            def y_turn(b, q, i):
                E_y.done(pe, q, i)
                E_f.before(pe, q, i)
                E_t.begin(pe, q, i)(turn(bank[q], flat(yt[q])))

            last_batches(pe, y_turn)


def kernel(**inputs):
    import concourse.bacc as bacc
    from concourse import mybir
    from concourse.bass_utils import run_bass_kernel_spmd

    def t(name):
        return np.ascontiguousarray(np.asarray(inputs[name]).T)

    x = np.ascontiguousarray(inputs["L0_attn_x"])
    nb, nt, c = x.shape
    vecs = ["L0_attn_ln1_g", "L0_attn_ln1_b", "L0_attn_ln2_g", "L0_attn_ln2_b", "L0_attn_att_time_mix",
            "L0_attn_att_combined_mix", "L0_attn_time_decay", "L0_attn_time_first", "L0_attn_ffn_time_mix",
            "L0_attn_ffn_combined_mix"]
    arrays = {
        "x": x,
        "xT": np.ascontiguousarray(x.reshape(nb * nt, c).T),
        "vecs": np.ascontiguousarray(np.stack([np.asarray(inputs[n]).reshape(c) for n in vecs], axis=1)),
        "cT": t("L0_c"),
        "wmod": np.ascontiguousarray(inputs["L0_wmod"]),
        "WkT": t("L0_attn_Wk"), "WvT": t("L0_attn_Wv"), "WrT": t("L0_attn_Wr"), "WoT": t("L0_attn_Wo"),
        "FkT": t("L0_attn_Fk"), "FvT": t("L0_attn_Fv"), "FrT": t("L0_attn_Fr"),
        "routerT": t("L0_ffn_w_router"),
        "gateT": t("L0_ffn_w_gate"), "upT": t("L0_ffn_w_up"), "downT": t("L0_ffn_w_down"),
        "gate_up": np.ascontiguousarray(inputs["L0_ffn_gate_up_proj"]),
        "down": np.ascontiguousarray(inputs["L0_ffn_down_proj"]),
    }
    nc = bacc.Bacc("TRN2", target_bir_lowering=False, num_devices=1)
    ins = {n: nc.dram_tensor(f"in_{n}", a.shape, mybir.dt.float32, kind="ExternalInput").ap() for n, a in arrays.items()}
    out_t = nc.dram_tensor("out_t", (c, nb * nt), mybir.dt.float32, kind="ExternalOutput").ap()
    program(nc, ins, out_t)
    got = run_bass_kernel_spmd(nc, [{f"in_{n}": a for n, a in arrays.items()}], core_ids=[0])
    return np.ascontiguousarray(got.results[0]["out_t"].T).reshape(nb, nt, c)
```
